# Optimizing a Trainium2 kernel written in Bass

```python
import numpy as np
import jax
import jax.numpy as jnp

def _softmax(x, axis=-1):
    return jax.nn.softmax(x, axis=axis)

def _gelu(x):
    return jax.nn.gelu(x, approximate=True)

def _silu(x):
    return jax.nn.silu(x)

def _sigmoid(x):
    return jax.nn.sigmoid(x)

def _layernorm(x, axis=-1, eps=1e-05):
    m = jnp.mean(x, axis=axis, keepdims=True)
    v = jnp.var(x, axis=axis, keepdims=True)
    return (x - m) / jnp.sqrt(v + eps)

def _scatter_add(tgt, idx, src, axis=0):
    return tgt.at[idx].add(src)

def _segment_sum(src, seg, n):
    return jax.ops.segment_sum(src, seg, n)
kernel_name = 'mk_gps_d1_gnn_r8_e12f5e'

def setup_inputs(seed: int=0):
    np.random.seed(seed)
    _w = jnp.asarray

    def _rec_inputs():
        import jax
        import jax.numpy as jnp
        _gk = jax.random.key(seed)
        x = -0.0002117 + 1 * jax.random.normal(jax.random.fold_in(_gk, 1), (1250, 512), jnp.float32)
        _s = jax.random.randint(jax.random.fold_in(_gk, 2), (20000,), 0, 1250, jnp.int32)
        _d = jax.random.randint(jax.random.fold_in(_gk, 3), (20000,), 0, 1250, jnp.int32)
        _loop = jnp.arange(1250, dtype=jnp.int32)
        src = jnp.concatenate([_s, _d, _loop])
        dst = jnp.concatenate([_d, _s, _loop])
        _o = jnp.argsort(dst, stable=True)
        src = src[_o]
        dst = dst[_o]
        return (x, src, dst)
    x, src, dst = _rec_inputs()

    def _L0_gnn_setup():
        import jax, jax.numpy as jnp
        import numpy as np
        N_NODES = 6250
        N_EDGES = 100000
        D_IN = 512
        D_OUT = 512
        key = jax.random.key(seed)
        k1, k2, k3, k4, k5 = jax.random.split(key, 5)
        local_feats = jax.random.normal(k1, (N_NODES, D_IN), dtype=jnp.float32)
        src = jax.random.randint(k2, (N_EDGES,), 0, N_NODES, dtype=jnp.int64)
        dst = jax.random.randint(k3, (N_EDGES,), 0, N_NODES, dtype=jnp.int64)
        lim = (6.0 / (D_IN + D_OUT)) ** 0.5
        W_self = jax.random.uniform(k4, (D_OUT, D_IN), minval=-lim, maxval=lim, dtype=jnp.float32)
        W_neigh = jax.random.uniform(k5, (D_OUT, D_IN), minval=-lim, maxval=lim, dtype=jnp.float32)
        b = jnp.zeros((D_OUT,), dtype=jnp.float32)
        return {'local_feats': local_feats, 'src': src, 'dst': dst, 'layer': 0, 'W_self': W_self, 'W_neigh': W_neigh, 'b': b}
    _L0_gnn_all = _L0_gnn_setup()
    _L0_gnn_in = {k: v for k, v in _L0_gnn_all.items() if k in ('W_self', 'W_neigh', 'b')}
    del _L0_gnn_all

    def _L0_mix_setup():
        import jax, jax.numpy as jnp
        import numpy as np
        B, T, D, H = (4, 1024, 512, 8)
        HD = D // H
        key = jax.random.key(seed)
        k0, k1, k2 = jax.random.split(key, 3)
        std = 1.0 / np.sqrt(D)
        return {'x': jax.random.normal(k0, (B, T, D), dtype=jnp.float32), 'W_qkv': jax.random.normal(k1, (3 * D, D), dtype=jnp.float32) * std, 'b_qkv': jnp.zeros((3 * D,), dtype=jnp.float32), 'W_out': jax.random.normal(k2, (D, D), dtype=jnp.float32) * std, 'b_out': jnp.zeros((D,), dtype=jnp.float32)}
    _L0_mix_all = _L0_mix_setup()
    _L0_mix_in = {k: v for k, v in _L0_mix_all.items() if k in ('W_qkv', 'b_qkv', 'W_out', 'b_out')}
    del _L0_mix_all

    def _L0_ffn_setup():
        import jax, jax.numpy as jnp
        import numpy as np
        D = 512
        H = 8
        K = 4
        HD = D // H

        def _ln(x, w, b, eps=1e-05):
            m = x.mean(-1, keepdims=True)
            v = ((x - m) ** 2).mean(-1, keepdims=True)
            return (x - m) / jnp.sqrt(v + eps) * w + b

        def _spatial_experts(xn, idx, in_w, in_b, out_w, out_b):
            W = in_w[idx]
            qkv = jnp.einsum('btd,bed->bte', xn, W) + in_b[idx][:, None, :]
            q, k, v = jnp.split(qkv, 3, axis=-1)
            B, T, _ = xn.shape
            q = q.reshape(B, T, H, HD) * HD ** (-0.5)
            k = k.reshape(B, T, H, HD)
            v = v.reshape(B, T, H, HD)
            att = jax.nn.softmax(jnp.einsum('bthd,bshd->bhts', q, k), axis=-1)
            o = jnp.einsum('bhts,bshd->bthd', att, v).reshape(B, T, D)
            return jnp.einsum('btd,bod->bto', o, out_w[idx]) + out_b[idx][:, None, :]

        def _temporal_experts(xt, idx, qw, qb, kw, kb, vw, vb, pw, pb):
            B, T, _ = xt.shape
            q = (jnp.einsum('btd,bod->bto', xt, qw[idx]) + qb[idx][:, None, :]).reshape(B, T, H, HD)
            k = (jnp.einsum('btd,bod->bto', xt, kw[idx]) + kb[idx][:, None, :]).reshape(B, T, H, HD)
            v = (jnp.einsum('btd,bod->bto', xt, vw[idx]) + vb[idx][:, None, :]).reshape(B, T, H, HD)
            logits = jnp.einsum('bthd,bshd->bhts', q, k) * HD ** (-0.5)
            causal = jnp.tril(jnp.ones((T, T), dtype=bool))
            logits = jnp.where(causal, logits, -jnp.inf)
            att = jax.nn.softmax(logits, axis=-1)
            o = jnp.einsum('bhts,bshd->bthd', att, v).reshape(B, T, D)
            o = jnp.einsum('btd,bod->bto', o, pw[idx]) + pb[idx][:, None, :]
            return xt + o

        def _cross_mha(q_in, kv_in, in_w, in_b, out_w, out_b):
            B, T, _ = q_in.shape
            S = kv_in.shape[1]
            Wq, Wk, Wv = (in_w[:D], in_w[D:2 * D], in_w[2 * D:])
            bq, bk, bv = (in_b[:D], in_b[D:2 * D], in_b[2 * D:])
            q = (q_in @ Wq.T + bq).reshape(B, T, H, HD) * HD ** (-0.5)
            k = (kv_in @ Wk.T + bk).reshape(B, S, H, HD)
            v = (kv_in @ Wv.T + bv).reshape(B, S, H, HD)
            att = jax.nn.softmax(jnp.einsum('bthd,bshd->bhts', q, k), axis=-1)
            o = jnp.einsum('bhts,bshd->bthd', att, v).reshape(B, T, D)
            return o @ out_w.T + out_b
        key = jax.random.key(seed)
        ks = iter(jax.random.split(key, 40))
        B, T = (256, 64)
        p = lambda *shape: jax.random.normal(next(ks), shape, dtype=jnp.float32) * 0.02
        inp = {'x': jax.random.normal(next(ks), (B, T, D), dtype=jnp.float32), 'router_w1': p(128, D), 'router_b1': jnp.zeros((128,), jnp.float32), 'router_w2': p(2 * K, 128), 'router_b2': jnp.zeros((2 * K,), jnp.float32), 'norm_s_w': jnp.ones((D,), jnp.float32), 'norm_s_b': jnp.zeros((D,), jnp.float32), 'norm_t_w': jnp.ones((D,), jnp.float32), 'norm_t_b': jnp.zeros((D,), jnp.float32), 'sp_in_w': p(K, 3 * D, D), 'sp_in_b': jnp.zeros((K, 3 * D), jnp.float32), 'sp_out_w': p(K, D, D), 'sp_out_b': jnp.zeros((K, D), jnp.float32), 'tq_w': p(K, D, D), 'tq_b': jnp.zeros((K, D), jnp.float32), 'tk_w': p(K, D, D), 'tk_b': jnp.zeros((K, D), jnp.float32), 'tv_w': p(K, D, D), 'tv_b': jnp.zeros((K, D), jnp.float32), 'tp_w': p(K, D, D), 'tp_b': jnp.zeros((K, D), jnp.float32), 'cross_in_w': p(3 * D, D), 'cross_in_b': jnp.zeros((3 * D,), jnp.float32), 'cross_out_w': p(D, D), 'cross_out_b': jnp.zeros((D,), jnp.float32), 'norm_mlp_w': jnp.ones((D,), jnp.float32), 'norm_mlp_b': jnp.zeros((D,), jnp.float32), 'mlp_w1': p(4 * D, D), 'mlp_b1': jnp.zeros((4 * D,), jnp.float32), 'mlp_w2': p(D, 4 * D), 'mlp_b2': jnp.zeros((D,), jnp.float32)}
        return inp
    _L0_ffn_all = _L0_ffn_setup()
    _L0_ffn_in = {k: v for k, v in _L0_ffn_all.items() if k in ('router_w1', 'router_b1', 'router_w2', 'router_b2', 'norm_s_w', 'norm_s_b', 'norm_t_w', 'norm_t_b', 'sp_in_w', 'sp_in_b', 'sp_out_w', 'sp_out_b', 'tq_w', 'tq_b', 'tk_w', 'tk_b', 'tv_w', 'tv_b', 'tp_w', 'tp_b', 'cross_in_w', 'cross_in_b', 'cross_out_w', 'cross_out_b', 'norm_mlp_w', 'norm_mlp_b', 'mlp_w1', 'mlp_b1', 'mlp_w2', 'mlp_b2')}
    del _L0_ffn_all
    return {'x': x, 'src': src, 'dst': dst, 'L0_gnn_W_self': _L0_gnn_in['W_self'], 'L0_gnn_W_neigh': _L0_gnn_in['W_neigh'], 'L0_gnn_b': _L0_gnn_in['b'], 'L0_mix_W_qkv': _L0_mix_in['W_qkv'], 'L0_mix_b_qkv': _L0_mix_in['b_qkv'], 'L0_mix_W_out': _L0_mix_in['W_out'], 'L0_mix_b_out': _L0_mix_in['b_out'], 'L0_ffn_router_w1': _L0_ffn_in['router_w1'], 'L0_ffn_router_b1': _L0_ffn_in['router_b1'], 'L0_ffn_router_w2': _L0_ffn_in['router_w2'], 'L0_ffn_router_b2': _L0_ffn_in['router_b2'], 'L0_ffn_norm_s_w': _L0_ffn_in['norm_s_w'], 'L0_ffn_norm_s_b': _L0_ffn_in['norm_s_b'], 'L0_ffn_norm_t_w': _L0_ffn_in['norm_t_w'], 'L0_ffn_norm_t_b': _L0_ffn_in['norm_t_b'], 'L0_ffn_sp_in_w': _L0_ffn_in['sp_in_w'], 'L0_ffn_sp_in_b': _L0_ffn_in['sp_in_b'], 'L0_ffn_sp_out_w': _L0_ffn_in['sp_out_w'], 'L0_ffn_sp_out_b': _L0_ffn_in['sp_out_b'], 'L0_ffn_tq_w': _L0_ffn_in['tq_w'], 'L0_ffn_tq_b': _L0_ffn_in['tq_b'], 'L0_ffn_tk_w': _L0_ffn_in['tk_w'], 'L0_ffn_tk_b': _L0_ffn_in['tk_b'], 'L0_ffn_tv_w': _L0_ffn_in['tv_w'], 'L0_ffn_tv_b': _L0_ffn_in['tv_b'], 'L0_ffn_tp_w': _L0_ffn_in['tp_w'], 'L0_ffn_tp_b': _L0_ffn_in['tp_b'], 'L0_ffn_cross_in_w': _L0_ffn_in['cross_in_w'], 'L0_ffn_cross_in_b': _L0_ffn_in['cross_in_b'], 'L0_ffn_cross_out_w': _L0_ffn_in['cross_out_w'], 'L0_ffn_cross_out_b': _L0_ffn_in['cross_out_b'], 'L0_ffn_norm_mlp_w': _L0_ffn_in['norm_mlp_w'], 'L0_ffn_norm_mlp_b': _L0_ffn_in['norm_mlp_b'], 'L0_ffn_mlp_w1': _L0_ffn_in['mlp_w1'], 'L0_ffn_mlp_b1': _L0_ffn_in['mlp_b1'], 'L0_ffn_mlp_w2': _L0_ffn_in['mlp_w2'], 'L0_ffn_mlp_b2': _L0_ffn_in['mlp_b2']}

def reference(x, src, dst, L0_gnn_W_self, L0_gnn_W_neigh, L0_gnn_b, L0_mix_W_qkv, L0_mix_b_qkv, L0_mix_W_out, L0_mix_b_out, L0_ffn_router_w1, L0_ffn_router_b1, L0_ffn_router_w2, L0_ffn_router_b2, L0_ffn_norm_s_w, L0_ffn_norm_s_b, L0_ffn_norm_t_w, L0_ffn_norm_t_b, L0_ffn_sp_in_w, L0_ffn_sp_in_b, L0_ffn_sp_out_w, L0_ffn_sp_out_b, L0_ffn_tq_w, L0_ffn_tq_b, L0_ffn_tk_w, L0_ffn_tk_b, L0_ffn_tv_w, L0_ffn_tv_b, L0_ffn_tp_w, L0_ffn_tp_b, L0_ffn_cross_in_w, L0_ffn_cross_in_b, L0_ffn_cross_out_w, L0_ffn_cross_out_b, L0_ffn_norm_mlp_w, L0_ffn_norm_mlp_b, L0_ffn_mlp_w1, L0_ffn_mlp_b1, L0_ffn_mlp_w2, L0_ffn_mlp_b2):
    import jax
    import jax.numpy as jnp

    def _L0_gnn_ref(local_feats, src, dst, layer, W_self, W_neigh, b):
        import jax, jax.numpy as jnp
        import numpy as np
        N_NODES = 6250
        N_EDGES = 100000
        D_IN = 512
        D_OUT = 512
        'DistSAGEConv forward: mean neighbor aggregation + fc_self + fc_neigh + bias + ReLU.\n            `layer` only selects which hop in the distributed impl; aggregation math is identical.\n            '
        n = local_feats.shape[0]
        msg = local_feats[src]
        agg = jax.ops.segment_sum(msg, dst, num_segments=n)
        deg = jax.ops.segment_sum(jnp.ones((src.shape[0],), local_feats.dtype), dst, num_segments=n)
        h_neigh = agg / jnp.maximum(deg, 1.0)[:, None]
        rst = local_feats @ W_self.T + h_neigh @ W_neigh.T + b
        return jax.nn.relu(rst)

    def _L0_mix_ref(x, W_qkv, b_qkv, W_out, b_out):
        import jax, jax.numpy as jnp
        import numpy as np
        B, T, D, H = (4, 1024, 512, 8)
        HD = D // H
        b, t, d = x.shape
        qkv = x @ W_qkv.T + b_qkv
        q, k, v = jnp.split(qkv, 3, axis=-1)

        def to_heads(u):
            return u.reshape(b, t, H, HD).transpose(0, 2, 1, 3)
        q, k, v = (to_heads(q), to_heads(k), to_heads(v))
        k = jax.nn.softmax(k, axis=-2)
        context = jnp.einsum('bhtd,bhtv->bhdv', k, v)
        out = jnp.einsum('bhtd,bhdv->bhtv', q, context)
        out = out.transpose(0, 2, 1, 3).reshape(b, t, d)
        return out @ W_out.T + b_out

    def _L0_ffn_ref(x, router_w1, router_b1, router_w2, router_b2, norm_s_w, norm_s_b, norm_t_w, norm_t_b, sp_in_w, sp_in_b, sp_out_w, sp_out_b, tq_w, tq_b, tk_w, tk_b, tv_w, tv_b, tp_w, tp_b, cross_in_w, cross_in_b, cross_out_w, cross_out_b, norm_mlp_w, norm_mlp_b, mlp_w1, mlp_b1, mlp_w2, mlp_b2):
        import jax, jax.numpy as jnp
        import numpy as np
        D = 512
        H = 8
        K = 4
        HD = D // H

        def _ln(x, w, b, eps=1e-05):
            m = x.mean(-1, keepdims=True)
            v = ((x - m) ** 2).mean(-1, keepdims=True)
            return (x - m) / jnp.sqrt(v + eps) * w + b

        def _spatial_experts(xn, idx, in_w, in_b, out_w, out_b):
            W = in_w[idx]
            qkv = jnp.einsum('btd,bed->bte', xn, W) + in_b[idx][:, None, :]
            q, k, v = jnp.split(qkv, 3, axis=-1)
            B, T, _ = xn.shape
            q = q.reshape(B, T, H, HD) * HD ** (-0.5)
            k = k.reshape(B, T, H, HD)
            v = v.reshape(B, T, H, HD)
            att = jax.nn.softmax(jnp.einsum('bthd,bshd->bhts', q, k), axis=-1)
            o = jnp.einsum('bhts,bshd->bthd', att, v).reshape(B, T, D)
            return jnp.einsum('btd,bod->bto', o, out_w[idx]) + out_b[idx][:, None, :]

        def _temporal_experts(xt, idx, qw, qb, kw, kb, vw, vb, pw, pb):
            B, T, _ = xt.shape
            q = (jnp.einsum('btd,bod->bto', xt, qw[idx]) + qb[idx][:, None, :]).reshape(B, T, H, HD)
            k = (jnp.einsum('btd,bod->bto', xt, kw[idx]) + kb[idx][:, None, :]).reshape(B, T, H, HD)
            v = (jnp.einsum('btd,bod->bto', xt, vw[idx]) + vb[idx][:, None, :]).reshape(B, T, H, HD)
            logits = jnp.einsum('bthd,bshd->bhts', q, k) * HD ** (-0.5)
            causal = jnp.tril(jnp.ones((T, T), dtype=bool))
            logits = jnp.where(causal, logits, -jnp.inf)
            att = jax.nn.softmax(logits, axis=-1)
            o = jnp.einsum('bhts,bshd->bthd', att, v).reshape(B, T, D)
            o = jnp.einsum('btd,bod->bto', o, pw[idx]) + pb[idx][:, None, :]
            return xt + o

        def _cross_mha(q_in, kv_in, in_w, in_b, out_w, out_b):
            B, T, _ = q_in.shape
            S = kv_in.shape[1]
            Wq, Wk, Wv = (in_w[:D], in_w[D:2 * D], in_w[2 * D:])
            bq, bk, bv = (in_b[:D], in_b[D:2 * D], in_b[2 * D:])
            q = (q_in @ Wq.T + bq).reshape(B, T, H, HD) * HD ** (-0.5)
            k = (kv_in @ Wk.T + bk).reshape(B, S, H, HD)
            v = (kv_in @ Wv.T + bv).reshape(B, S, H, HD)
            att = jax.nn.softmax(jnp.einsum('bthd,bshd->bhts', q, k), axis=-1)
            o = jnp.einsum('bhts,bshd->bthd', att, v).reshape(B, T, D)
            return o @ out_w.T + out_b
        pooled = x.mean(axis=1)
        h = jax.nn.gelu(pooled @ router_w1.T + router_b1, approximate=False)
        route = jax.nn.softmax(h @ router_w2.T + router_b2, axis=-1)
        idx_s = jnp.argmax(route[:, :K], axis=-1)
        idx_t = jnp.argmax(route[:, K:], axis=-1)
        xn = _ln(x, norm_s_w, norm_s_b)
        spatial_out = _spatial_experts(xn, idx_s, sp_in_w, sp_in_b, sp_out_w, sp_out_b)
        xt = _ln(x, norm_t_w, norm_t_b)
        temporal_out = _temporal_experts(xt, idx_t, tq_w, tq_b, tk_w, tk_b, tv_w, tv_b, tp_w, tp_b)
        fused = _cross_mha(spatial_out, temporal_out, cross_in_w, cross_in_b, cross_out_w, cross_out_b)
        x = x + fused
        h2 = _ln(x, norm_mlp_w, norm_mlp_b)
        x = x + (jax.nn.gelu(h2 @ mlp_w1.T + mlp_b1, approximate=False) @ mlp_w2.T + mlp_b2)
        return x
    xn = _layernorm(x, axis=-1)
    x = x + _L0_gnn_ref(xn, src, dst, 0, L0_gnn_W_self, L0_gnn_W_neigh, L0_gnn_b) + _L0_mix_ref(xn[None], L0_mix_W_qkv, L0_mix_b_qkv, L0_mix_W_out, L0_mix_b_out)[0]
    x = x + _L0_ffn_ref(_layernorm(x, axis=-1)[None], L0_ffn_router_w1, L0_ffn_router_b1, L0_ffn_router_w2, L0_ffn_router_b2, L0_ffn_norm_s_w, L0_ffn_norm_s_b, L0_ffn_norm_t_w, L0_ffn_norm_t_b, L0_ffn_sp_in_w, L0_ffn_sp_in_b, L0_ffn_sp_out_w, L0_ffn_sp_out_b, L0_ffn_tq_w, L0_ffn_tq_b, L0_ffn_tk_w, L0_ffn_tk_b, L0_ffn_tv_w, L0_ffn_tv_b, L0_ffn_tp_w, L0_ffn_tp_b, L0_ffn_cross_in_w, L0_ffn_cross_in_b, L0_ffn_cross_out_w, L0_ffn_cross_out_b, L0_ffn_norm_mlp_w, L0_ffn_norm_mlp_b, L0_ffn_mlp_w1, L0_ffn_mlp_b1, L0_ffn_mlp_w2, L0_ffn_mlp_b2)[0]
    return x

_drawn_inputs = setup_inputs


def setup_inputs(seed=0):
    import zlib

    import numpy as np

    out = dict(_drawn_inputs(seed))
    spreads = {'L0_gnn_b': (0.0, 0.8),
     'L0_mix_b_qkv': (0.0, 0.1),
     'L0_mix_b_out': (0.0, 0.773),
     'L0_ffn_router_b1': (0.0, 0.1),
     'L0_ffn_router_b2': (0.0, 0.8),
     'L0_ffn_norm_s_w': (1.0, 0.6),
     'L0_ffn_norm_s_b': (0.0, 0.8),
     'L0_ffn_norm_t_w': (1.0, 0.6),
     'L0_ffn_norm_t_b': (0.0, 0.8),
     'L0_ffn_sp_in_b': (0.0, 0.8),
     'L0_ffn_sp_out_b': (0.0, 0.8),
     'L0_ffn_tq_b': (0.0, 0.8),
     'L0_ffn_tk_b': (0.0, 2.0),
     'L0_ffn_tv_b': (0.0, 0.8),
     'L0_ffn_tp_b': (0.0, 0.8),
     'L0_ffn_cross_in_b': (0.0, 0.8),
     'L0_ffn_cross_out_b': (0.0, 2.0),
     'L0_ffn_norm_mlp_w': (1.0, 0.6),
     'L0_ffn_norm_mlp_b': (0.0, 2.0),
     'L0_ffn_mlp_b1': (0.0, 2.0),
     'L0_ffn_mlp_b2': (0.0, 2.0)}
    factors = {'L0_gnn_W_neigh': 4.438,
     'L0_ffn_router_w1': 8.0,
     'L0_ffn_sp_in_w': 8.0,
     'L0_ffn_sp_out_w': 8.0,
     'L0_ffn_tq_w': 8.0,
     'L0_ffn_tk_w': 8.0,
     'L0_ffn_tv_w': 8.0,
     'L0_ffn_tp_w': 8.0,
     'L0_ffn_cross_in_w': 8.0,
     'L0_ffn_cross_out_w': 8.0,
     'L0_ffn_mlp_w1': 8.0,
     'L0_ffn_mlp_w2': 8.0}
    for name, (base, spread) in spreads.items():
        noise = np.random.default_rng([zlib.crc32(name.encode()), seed]).standard_normal(out[name].shape)
        drawn = base * np.exp(spread * noise) if base else spread * noise
        out[name] = jnp.asarray(drawn.astype(out[name].dtype))
    for name, factor in factors.items():
        out[name] = (out[name] * factor).astype(out[name].dtype)
    return out
```

```python
import numpy as np
from contextlib import ExitStack

import concourse.bass as bass
from concourse import mybir

F32 = mybir.dt.float32
F32R = mybir.dt.float32r
F16 = mybir.dt.float16
BF16 = mybir.dt.bfloat16
I32 = mybir.dt.int32
ACT = mybir.ActivationFunctionType
ALU = mybir.AluOpType
AX = mybir.AxisListType

NODES, D, HEADS, EXPERTS = 1250, 512, 8, 4
HD = D // HEADS
SCALE = HD ** -0.5
TOK = 125
NT = NODES // TOK
FB = D // 128
NP = 418
TP = 3 * NP
EDGES = 2 * 20000 + NODES
ET = 125
CH = 3
NCH = EDGES // (ET * CH)
EPC = ET * CH
WIN = 32
NW = 40
DH = NT * WIN
WSHIFT = 512
MAGIC = 12582912.0
NEG = -3.0e38
EPS = 1e-5
MLPQ = 4
BLK = FB * 128

V_GNN, V_MIX, V_MIXO = 0, 4, 16
V_SW, V_SB, V_TW, V_TB = 20, 24, 28, 32
V_CIN, V_COUT, V_MW, V_MB, V_M1, V_M2, V_R1 = 36, 48, 52, 56, 60, 76, 80
NVEC = 81


def slots_of(lengths):
    out = []
    for n in lengths:
        out += [r % 3 for r in range(n)]
    return out


STRETCH = [8] + [3] * 4 + [4] + ([3] * 4 + [4]) * 3 + [8] * 4
SLOTS = slots_of(STRETCH)


def since(k):
    for d in range(1, k + 1):
        if SLOTS[k - d] == SLOTS[k]:
            return d
    return None


def since_in_loop(base, length, passes, r):
    return min(since(base + length * i + r) for i in range(passes))


W_GNN, W_MIX, W_MIXO = 0, 8, 20
W_SP, W_TP, W_CR, W_MLP = 24, 40, 56, 72
assert len(SLOTS) == W_MLP + 32

PROBS, PT = 4, 4
ROUTE_STEPS = 10
EDGE_KEYS, EDGE_INSIDE, EDGE_BOUNDS, EDGE_DONE = 9, 21, 25, 28
AGG_OF, AGG_BANK = [0, 2, 3, 4], [0, 0, 3, 0]

RING = 5


def score_plan(causal):
    plan, at = [], 0
    for n in range(2 * NT):
        g = (n % NT) // 2
        width = 2 * TOK * (g + 1) if causal else NODES
        count = -(-width // 512)
        banks = [(at + j) % RING for j in range(count)]
        if count == 3:
            odd = 2 if banks[2] == 0 else 0
            sizes = [418 if j == odd else 416 for j in range(3)]
        elif count == 2:
            sizes = [width // 2 // 2 * 2, width - width // 2 // 2 * 2]
        else:
            sizes = [width]
        first = [sum(sizes[:j]) for j in range(count)]
        pieces = list(zip(banks, first, sizes))
        plan.append((width, pieces))
        at = (at + count) % RING
    return plan


def runs_of(pieces):
    runs = []
    for bank, first, n in pieces:
        if runs and runs[-1][0] + runs[-1][1] == bank and runs[-1][3] == n:
            runs[-1][1] += 1
        else:
            runs.append([bank, 1, first, n])
    return runs



def build(nc, A, out):
    ctx = ExitStack()
    with ctx:
        def sem(name):
            return ctx.enter_context(nc.semaphore(name))

        place = {"end": -(-nc.sbuf_base // 64) * 64}

        def sb(name, shape, dt, pos=None):
            pos = place["end"] if pos is None else pos
            size = 2 if dt in (F16, BF16) else 4
            for s in shape[1:]:
                size *= s
            place["end"] = pos + -(-size // 64) * 64
            assert place["end"] <= nc.sbuf_usable_end, name
            return nc.alloc_sbuf_tensor_at(name, shape, dt, offset=pos)

        ident = sb("ident", [128, 128], F32)
        identb = sb("identb", [128, 128], BF16)
        causal_mask = sb("causal_mask", [TOK, 3 * TOK], BF16)
        vecs = sb("vecs", [128, NVEC], F32)
        sp_vecs = sb("sp_vecs", [128, 16], F32)
        tp_vecs = sb("tp_vecs", [128, 16], F32)
        small = sb("small", [128, 8], F32)
        pool_tick = sb("pool_tick", [128, 24], F32)
        w_raw = sb("w_raw", [128, 3, BLK], F32)
        w_hi = sb("w_hi", [128, 3, BLK], F32R)
        w_lo = sb("w_lo", [128, 3, BLK], F32R)
        xa_at = place["end"]
        xa_hi = sb("xa_hi", [128, FB, TP], F32R)
        xa_lo = sb("xa_lo", [128, FB, TP], F32R)
        xb_at = place["end"]
        xb_hi = sb("xb_hi", [128, FB, TP], F32R)
        xb_lo = sb("xb_lo", [128, FB, TP], F32R)
        feat_at = place["end"]
        feat = sb("feat", [128, FB, TP], F32)
        work_at = place["end"]

        tok_a = sb("tok_a", [TOK, NT, D], F32, work_at)
        tok_b_at = place["end"]
        adj = sb("adj", [TOK, NT, NW * WIN], F32)
        onehot = sb("onehot", [ET, 2 * CH, ET + DH], F16)
        src_i = sb("src_i", [NCH, EPC], I32, xb_at)
        dst_i = sb("dst_i", [NCH, EPC], I32)
        src_f = sb("src_f", [NCH, EPC], F32)
        dst_f = sb("dst_f", [NCH, EPC], F32)
        src_tile = sb("src_tile", [NCH, EPC], F32)
        src_low = sb("src_low", [NCH, EPC], F32)
        dst_win = sb("dst_win", [NCH, EPC], F32)
        edge_key = sb("edge_key", [NCH, EPC], F32)
        low_t = sb("low_t", [ET, NCH, CH], F32)
        key_t = sb("key_t", [ET, NCH, CH], F32)
        iota_i = sb("iota_i", [128, DH], I32)
        iota_h = sb("iota_h", [128, DH], F16)
        win_i = sb("win_i", [128, NW], I32)
        win_no = sb("win_no", [128, NW], F32)
        win_key = sb("win_key", [128, NW], F32)
        chunk_i = sb("chunk_i", [128, 1], I32)
        chunk_f = sb("chunk_f", [128, 4], F32)
        inside = sb("inside", [NCH, 3, NW], F32)
        bounds_c = sb("bounds_c", [NW, 2], F32)
        bounds_r = sb("bounds_r", [1, 2, NW], F32)
        bounds_i = sb("bounds_i", [1, 2 * NW], I32)
        assert place["end"] <= feat_at
        deg_part = sb("deg_part", [TOK, NW * WIN], F32, feat_at)
        inv_deg = sb("inv_deg", [128, TP], F32)
        agg_tmp = sb("agg_tmp", [128, TP], F32)
        ones = sb("ones", [128, 128], F32)
        assert place["end"] <= work_at

        mix_q = sb("mix_q", [128, TP], F32, work_at)
        mix_k = sb("mix_k", [128, TP], F32)
        mix_v = sb("mix_v", [128, TP], F32)
        mix_kt = sb("mix_kt", [TOK, NT, 128], F32)
        mix_vt = sb("mix_vt", [TOK, NT, 128], F32)
        context = sb("context", [128, 128], F32)

        x_again = sb("x_again", [TOK, NT, D], F32, xa_at)
        assert place["end"] <= xb_at
        tok_b = sb("tok_b", [TOK, NT, D], F32, tok_b_at)
        norm_tmp = sb("norm_tmp", [128, 2, 4 * TOK], F32)
        ln_stats = sb("ln_stats", [TOK, NT, 6], F32)
        ln_mv = sb("ln_mv", [TOK, NT, 2], F32)
        ln_r = sb("ln_r", [TOK, 4, NT], F32)
        router_w1 = sb("router_w1", [128, FB, 128], F32)
        router_w2 = sb("router_w2", [128, 2 * EXPERTS], F32)
        router_b2 = sb("router_b2", [1, 2 * EXPERTS], F32)
        mean_col = sb("mean_col", [TOK, 1], F32)
        pooled = sb("pooled", [128, FB], F32)
        route = sb("route", [1, 64], F32)
        expert_no = sb("expert_no", [1, 2 * EXPERTS], F32)
        expert_no_i = sb("expert_no_i", [1, 2 * EXPERTS], I32)
        route_i = sb("route_i", [1, 2], I32)
        mlp_tmp = sb("mlp_tmp", [128, 2, TP], F32)

        xc_hi = sb("xc_hi", [128, FB, TP], F32R, work_at)
        xc_lo = sb("xc_lo", [128, FB, TP], F32R)
        proj_tmp = sb("proj_tmp", [128, TP], F32)
        q_stack = sb("q_stack", [128, 2, TP], F32R, work_at)
        k_hi = sb("k_hi", [128, 2, TP], F32R)
        k_lo = sb("k_lo", [128, 2, TP], F32R)
        v_feat = sb("v_feat", [128, TP], F32)
        v_tok = sb("v_tok", [TOK, NT, 2, 128], F32R)
        probs = sb("probs", [TOK, PROBS, NODES], F32)
        pt_hi = sb("pt_hi", [TOK, PT, 4 * TOK], F32R)
        pt_lo = sb("pt_lo", [TOK, PT, 4 * TOK], F32R)
        o_half = sb("o_half", [128, 2 * TOK], F32)
        stats = sb("stats", [TOK, PROBS, 8], F32)

        ps = ctx.enter_context(nc.psum_tensor("ps", [128, 8, 512], F32))

        d_x1 = nc.dram_tensor("d_x1", [TOK, NT, D], F32, kind="Internal").ap()
        d_xn = nc.dram_tensor("d_xn", [TOK, NT, D], F32, kind="Internal").ap()
        d_xt = nc.dram_tensor("d_xt", [2, 128, FB, TP], F32, kind="Internal").ap()

        s_const = sem("s_const")
        s_constv = sem("s_constv")
        s_ld_x = sem("s_ld_x")
        s_ld_edge = sem("s_ld_edge")
        s_ld_vec = sem("s_ld_vec")
        s_ld_router = sem("s_ld_router")
        s_w_raw = [sem(f"s_w_raw{i}") for i in range(3)]
        s_w_split = sem("s_w_split")
        s_w_hi = sem("s_w_hi")
        s_w_used = sem("s_w_used")
        s_tr = sem("s_tr")
        s_tr_act = sem("s_tr_act")
        s_tr_dve = sem("s_tr_dve")
        s_ln = sem("s_ln")
        s_ln_sqrt = sem("s_ln_sqrt")
        s_ln_done = sem("s_ln_done")
        s_tmp = sem("s_tmp")
        s_edge = sem("s_edge")
        s_edge_tr = sem("s_edge_tr")
        s_hot = sem("s_hot")
        s_hot_free = sem("s_hot_free")
        s_win = sem("s_win")
        s_win_free = sem("s_win_free")
        s_agg = sem("s_agg")
        s_agg_dve = sem("s_agg_dve")
        s_agg_act = sem("s_agg_act")
        s_gnn = sem("s_gnn")
        s_mk = sem("s_mk")
        s_mq = sem("s_mq")
        s_mv = sem("s_mv")
        s_mmax = sem("s_mmax")
        s_mexp = sem("s_mexp")
        s_mrecip = sem("s_mrecip")
        s_mtr = sem("s_mtr")
        s_mk_out = sem("s_mk_out")
        s_mv_out = sem("s_mv_out")
        s_ctx = sem("s_ctx")
        s_ctx_out = sem("s_ctx_out")
        s_mo = sem("s_mo")
        s_mo_act = sem("s_mo_act")
        s_mo_dve = sem("s_mo_dve")
        s_mixout = sem("s_mixout")
        s_x1 = sem("s_x1")
        s_st = sem("s_st")
        s_st_xn = sem("s_st_xn")
        s_x_again = sem("s_x_again")
        s_xn_back = sem("s_xn_back")
        s_x1_back = sem("s_x1_back")
        s_xt_st = sem("s_xt_st")
        s_xt_ld = sem("s_xt_ld")
        s_pool_mm = sem("s_pool_mm")
        s_route = sem("s_route")
        s_route_act = sem("s_route_act")
        s_ld_ev = sem("s_ld_ev")
        s_k_hi = sem("s_k_hi")
        s_k_lo = sem("s_k_lo")
        s_k_half = sem("s_k_half")
        s_q_hi = sem("s_q_hi")
        s_q_lo = sem("s_q_lo")
        s_v = sem("s_v")
        s_vtr = sem("s_vtr")
        s_v_hi = sem("s_v_hi")
        s_v_lo = sem("s_v_lo")
        s_score = sem("s_score")
        s_mx = sem("s_mx")
        s_rowmax = sem("s_rowmax")
        s_exp = sem("s_exp")
        s_sum = sem("s_sum")
        s_recip = sem("s_recip")
        s_prob = sem("s_prob")
        s_pt = sem("s_pt")
        s_pt_hi = sem("s_pt_hi")
        s_pt_lo = sem("s_pt_lo")
        s_pv = sem("s_pv")
        s_o_half = sem("s_o_half")
        s_o = sem("s_o")
        s_xc_hi = sem("s_xc_hi")
        s_xc_lo = sem("s_xc_lo")
        s_pj_a = sem("s_pj_a")
        s_pj_d = sem("s_pj_d")
        s_zero = sem("s_zero")
        s_b2 = sem("s_b2")
        s_gelu = sem("s_gelu")
        s_hid_hi = sem("s_hid_hi")
        s_hid = sem("s_hid")
        s_acc = sem("s_acc")
        s_sum2 = sem("s_sum2")
        s_final = sem("s_final")
        s_out = sem("s_out")

        f32 = lambda ap: ap.bitcast(F32)

        TR1 = 12
        TR2 = TR1 + NT
        TR3 = TR2 + 12
        TR4 = TR3 + NT
        TR5 = TR4 + 12
        TR6 = TR5 + NT
        GAP = {0: 0, TR2: NT, TR4: 2 * NT}
        TRD = {0: 0, TR2: 12, TR4: 24}
        TB = [(0, 4), (4, 4), (8, 2)]

        ATT = [
            ("sp", W_SP, False), ("tp", W_TP, True), ("cr", W_CR, False)]
        NBATCH = [2 * sum(g + 1 if c else 5 for g in range(5)) for _, _, c in ATT]
        BASE_B = [sum(4 * n for n in NBATCH[:a]) for a in range(3)]

        def batches(a):
            return [(g, b) for g in range(NT) for b in range(g % 5 + 1 if ATT[a][2] else 5)]

        def order(a, g):
            nb = g % 5 + 1 if ATT[a][2] else 5
            steps = [("t", b) for b in range(min(2, nb))]
            late = [n for n in (2 * g + 3, 2 * g + 4) if n < 2 * NT]
            for b in range(nb):
                if b in (0, 2) and late:
                    steps.append(("s", late.pop(0)))
                steps.append(("p", b))
                if b + 2 < nb:
                    steps.append(("t", b + 2))
            steps += [("s", n) for n in late]
            return steps

        block = ctx.enter_context(nc.Block())

        @block.sync
        def _(sp):
            sp.dma_start(src_i[:, :], A["src"].rearrange("(p e) -> p e", p=NCH)).then_inc(s_ld_edge, 16)
            sp.dma_start(dst_i[:, :], A["dst"].rearrange("(p e) -> p e", p=NCH)).then_inc(s_ld_edge, 16)
            x_dram = A["x"].rearrange("(t p) d -> p t d", p=TOK)
            sp.dma_start(tok_a[:, :, :], x_dram).then_inc(s_ld_x, 16)
            sp.dma_start(vecs[:, :], A["vecs"]).then_inc(s_ld_vec, 16)

            def weights(k, slot, ago, source):
                if ago is not None:
                    sp.wait_ge(s_w_split, k - ago + 1)
                sp.dma_start(w_raw[:, slot, :], source).then_inc(s_w_raw[slot], 16)

            def block_of(name, index):
                return A[name][bass.ds(index, 1), :, :].rearrange("o p n -> (o p) n")

            for j in range(8):
                weights(W_GNN + j, SLOTS[j], since(j), block_of("w_gnn", j))
            with sp.Fori(0, 4) as i:
                for r in range(3):
                    weights(W_MIX + 3 * i + r, r, since_in_loop(W_MIX, 3, 4, r), block_of("w_mix", 4 * r + i))
            for j in range(4):
                k = W_MIXO + j
                weights(k, SLOTS[k], since(k), block_of("w_mix", 12 + j))
            sp.wait_ge(s_w_used, W_MIXO)
            sp.dma_start(x_again[:, :, :], x_dram).then_inc(s_x_again, 16)
            sp.wait_ge(s_x1, NT)
            sp.dma_start(router_w1[:, :, :], A["router_w1"]).then_inc(s_ld_router, 16)
            sp.dma_start(router_w2[:, :], A["router_w2"]).then_inc(s_ld_router, 16)
            sp.dma_start(router_b2[:, :], A["router_b2"]).then_inc(s_ld_router, 16)
            sp.dma_start(d_x1, tok_a[:, :, :]).then_inc(s_st, 16)
            sp.wait_ge(s_ln_done, 2 * NT)
            sp.dma_start(d_xn, tok_b[:, :, :]).then_inc(s_st_xn, 16)

            sp.wait_ge(s_route, ROUTE_STEPS)
            e_sp = sp.value_load(route_i[0:1, 0:1], min_val=0, max_val=EXPERTS - 1)
            e_tp = sp.value_load(route_i[0:1, 1:2], min_val=0, max_val=EXPERTS - 1)
            expert_vec = lambda name, e: A[name][bass.ds(e, 1), :, :].rearrange("o p n -> (o p) n")
            sp.dma_start(sp_vecs[:, :], expert_vec("v_sp", e_sp)).then_inc(s_ld_ev, 16)
            sp.dma_start(tp_vecs[:, :], expert_vec("v_tp", e_tp)).then_inc(s_ld_ev, 16)
            for a, (name, base, _) in enumerate(ATT):
                first = {"sp": e_sp * 16, "tp": e_tp * 16, "cr": 0}[name]
                with sp.Fori(0, 4) as i:
                    for r in range(3):
                        weights(base + 3 * i + r, r, since_in_loop(base, 3, 4, r),
                                block_of("w_" + name, first + 4 * r + i))
                if a == 0:
                    sp.wait_ge(s_tr_act, 24)
                    sp.wait_ge(s_tmp, 24)
                    sp.dma_start(d_xt[0], f32(xb_hi[:, :, :])).then_inc(s_xt_st, 16)
                    sp.dma_start(d_xt[1], f32(xb_lo[:, :, :])).then_inc(s_xt_st, 16)
                for j in range(4):
                    k = base + 12 + j
                    weights(k, SLOTS[k], since(k), block_of("w_" + name, first + 12 + j))
                if a == 0:
                    sp.wait_ge(s_w_used, base + 12)
                    sp.wait_ge(s_xt_st, 32)
                    sp.dma_start(f32(xa_hi[:, :, :]), d_xt[0]).then_inc(s_xt_ld, 16)
                    sp.dma_start(f32(xa_lo[:, :, :]), d_xt[1]).then_inc(s_xt_ld, 16)
            sp.wait_ge(s_w_used, W_MLP)
            sp.wait_ge(s_st_xn, 16)
            sp.dma_start(tok_b[:, :, :], d_xn).then_inc(s_xn_back, 16)
            with sp.Fori(0, MLPQ) as i:
                for r in range(8):
                    weights(W_MLP + 8 * i + r, r % 3, since_in_loop(W_MLP, 8, 4, r), block_of("w_mlp", 8 * i + r))
            sp.wait_ge(s_tr, TR5)
            sp.wait_ge(s_st, 16)
            sp.dma_start(tok_b[:, :, :], d_x1).then_inc(s_x1_back, 16)
            out_dram = out.rearrange("(t p) d -> p t d", p=TOK)
            for t in range(0, NT, 2):
                sp.wait_ge(s_final, t + 2)
                sp.dma_start(out_dram[:, t:t + 2, :], tok_b[:, t:t + 2, :]).then_inc(s_out, 16)
            sp.wait_ge(s_out, 16 * NT // 2)

        @block.gpsimd
        def _(pool):
            pool.memset(ident[:, :], 0.0).then_inc(s_const, 1)
            pool.wait_ge(s_const, 1)
            pool.affine_select(out=ident[:, :], in_=ident[:, :], compare_op=ALU.not_equal, fill=1.0, base=0,
                               pattern=[[-1, 128]], channel_multiplier=1).then_inc(s_const, 1)
            pool.memset(causal_mask[:, :], 0.0).then_inc(s_const, 1)
            pool.wait_ge(s_const, 3)
            pool.affine_select(out=causal_mask[:, :], in_=causal_mask[:, :], compare_op=ALU.is_ge, fill=NEG, base=TOK,
                               pattern=[[-1, 3 * TOK]], channel_multiplier=1).then_inc(s_const, 1)
            pool.iota(iota_i[:, :], [[1, DH]], base=0, channel_multiplier=0).then_inc(s_const, 1)
            pool.iota(win_i[:, :], [[1, NW]], base=0, channel_multiplier=0).then_inc(s_const, 1)
            pool.iota(chunk_i[:, :], [[0, 1]], base=1, channel_multiplier=1).then_inc(s_const, 1)
            pool.memset(ones[:, :], 1.0).then_inc(s_const, 1)

            def carry_wait(column=20):
                pool.tensor_tensor(pool_tick[:, column:column + 1], pool_tick[:, 21:22], pool_tick[:, 22:23], ALU.add)

            pool.memset(pool_tick[:, :], 0.0).then_inc(s_const, 1)
            pool.wait_ge(s_const, 9)

            def split(k, slot, ago, count):
                pool.wait_ge(s_w_raw[slot], 16 * count)
                if ago is not None:
                    pool.wait_ge(s_w_used, k - ago + 1)
                carry_wait()
                pool.tensor_copy(w_hi[:, slot, :], w_raw[:, slot, :]).then_inc(s_w_hi, 1)
                pool.wait_ge(s_w_hi, k + 1)
                pool.tensor_tensor(w_lo[:, slot, :], w_raw[:, slot, :], f32(w_hi[:, slot, :]), ALU.subtract)\
                    .then_inc(s_w_split, 1)

            def nth(k):
                return SLOTS[:k + 1].count(SLOTS[k])

            def split_at(k):
                split(k, SLOTS[k], since(k), nth(k))

            def split_loop(base, length, i, r):
                per_pass = sum(x % 3 == r % 3 for x in range(length))
                split(base + length * i + r, r % 3, since_in_loop(base, length, 4, r), nth(base + r) + per_pass * i)

            for j in range(8):
                split_at(W_GNN + j)
            with pool.Fori(0, 4) as i:
                for r in range(3):
                    split_loop(W_MIX, 3, i, r)
            for j in range(4):
                split_at(W_MIXO + j)
            pool.wait_ge(s_x1, NT)
            pool.memset(mean_col[:, :], 1.0 / NODES).then_inc(s_const, 1)
            pool.iota(expert_no_i[:, :], [[0, 2], [1, EXPERTS]], base=-100, channel_multiplier=0).then_inc(s_const, 1)
            for a, (_, base, causal) in enumerate(ATT):
                plan = score_plan(causal)
                for r in range(3):
                    split_at(base + r)

                def prob(n, i):
                    pool.wait_ge(s_recip, 20 * (4 * a + i) + n + 1)
                    carry_wait(n)
                    p = probs[:, n % PROBS, 0:plan[n][0]]
                    pool.tensor_scalar(p, p, stats[:, n % PROBS, 7:8], 1.0, ALU.mult, ALU.mult).then_inc(s_prob, 1)

                with pool.Fori(0, 3) as i:
                    for n in range(10):
                        prob(n, i)
                    for r in range(3):
                        split_loop(base, 3, i + 1, r)
                    for n in range(10, 20):
                        prob(n, i)
                for n in range(10):
                    prob(n, 3)
                for j in range(3):
                    split_at(base + 12 + j)
                for n in range(10, 20):
                    prob(n, 3)
                split_at(base + 15)
            with pool.Fori(0, MLPQ) as i:
                for r in range(8):
                    split_loop(W_MLP, 8, i, r)

        @block.scalar
        def _(act):
            wide = lambda b: ps[:, b:b + 3, 0:NP]
            flat = lambda ap: ap.rearrange("p (a n) -> p a n", a=3)
            act.wait_ge(s_constv, 2)

            def ln_root(n):
                act.wait_ge(s_ln, 8 * n + 3)
                act.activation(ln_r[:, 1, :], ln_r[:, 0, :], ACT.Sqrt).then_inc(s_ln_sqrt, 1)

            def banks_to_feature(base, targets):
                m = base
                for t0, nt in TB:
                    for f in range(FB):
                        act.wait_ge(s_tr, m + 1)
                        for x, (dst, sc, bi) in enumerate(targets):
                            o = dst[:, f, t0 * TOK:(t0 + nt) * TOK]
                            src = ps[:, 6 + m % 2, 0:nt * TOK]
                            if sc is None:
                                ins = act.activation(o, src, ACT.Copy)
                            else:
                                ins = act.activation(o, src, ACT.Identity, scale=vecs[:, sc + f:sc + f + 1],
                                                     bias=vecs[:, bi + f:bi + f + 1])
                        ins.then_inc(s_tr_act, 1)
                        m += 1

            ln_root(0)
            banks_to_feature(0, [(xa_hi, None, None)])

            act.activation(small[:, 6:7], small[:, 5:6], ACT.Copy).then_inc(s_win_free, 2)
            with act.Fori(0, NW // 2) as w2:
                for par in range(2):
                    act.wait_ge(s_win, 2 * w2 + (par + 1))
                    act.activation(adj[:, :, bass.ds((2 * w2 + par) * WIN, WIN)],
                                   ps[0:TOK, par, 0:DH].rearrange("p (t d) -> p t d", d=WIN), ACT.Copy)\
                        .then_inc(s_win_free, 1)
            for f in range(FB):
                act.wait_ge(s_agg_dve, 4 + 2 * f)
                act.activation(xb_hi[:, f, :], agg_tmp[:, :], ACT.Copy).then_inc(s_agg_act, 1)
            act.wait_ge(s_ld_vec, 16)
            for j in range(FB):
                act.wait_ge(s_w_used, W_GNN + 2 * j + 2)
                if j == 0:
                    act.wait_ge(s_agg_dve, 11)
                act.activation(flat(feat[:, j, :]), wide(3 * (j % 2)), ACT.Relu, bias=vecs[:, V_GNN + j:V_GNN + j + 1])\
                    .then_inc(s_gnn, 1)

            with act.Fori(0, 4) as i:
                def mix_in(dst, bank, r, s):
                    act.wait_ge(s_w_used, W_MIX + 3 * i + (r + 1))
                    act.activation(flat(dst[:, :]), wide(bank), ACT.Identity,
                                   bias=vecs[:, bass.ds(V_MIX + 4 * r + i, 1)]).then_inc(s, 1)
                mix_in(mix_k, 0, 0, s_mk)
                mix_in(mix_q, 3, 1, s_mq)
                act.wait_ge(s_mmax, i + 1)
                act.activation(mix_k[:, 0:NODES], mix_k[:, 0:NODES], ACT.Exp, bias=small[:, 0:1],
                               accum_out=small[:, 1:2]).then_inc(s_mexp, 1)
                mix_in(mix_v, 0, 2, s_mv)
                for b, (t0, nt) in enumerate(TB):
                    act.wait_ge(s_mtr, 6 * i + (b + 1))
                    act.activation(mix_kt[:, t0:t0 + nt, :], ps[0:TOK, 6 + b % 2, 0:nt * 128]
                                   .rearrange("p (t d) -> p t d", d=128), ACT.Copy).then_inc(s_mk_out, 1)
                act.wait_ge(s_mo, i + 1)
                act.activation(flat(xb_hi[:, bass.ds(i, 1), :].rearrange("p o n -> p (o n)")), wide(0), ACT.Copy)\
                    .then_inc(s_mo_act, 1)

            ln_root(1)
            ln_root(2)
            act.wait_ge(s_pool_mm, 2)
            act.activation(small[:, 4:5], ps[:, 5, 8:9], ACT.Gelu, bias=vecs[:, V_R1:V_R1 + 1]).then_inc(s_route_act, 1)
            act.wait_ge(s_route, 3)
            act.activation(route[:, 16:24], route[:, 0:8], ACT.Exp, bias=route[:, 8:9], accum_out=route[:, 9:10])\
                .then_inc(s_route_act, 1)
            banks_to_feature(TR2, [(xa_hi, V_SW, V_SB), (xb_hi, V_TW, V_TB)])

            for a, (name, base, causal) in enumerate(ATT):
                plan = score_plan(causal)
                bias, b0 = {"sp": (sp_vecs, 0), "tp": (tp_vecs, 0), "cr": (vecs, V_CIN)}[name]
                if a == 0:
                    act.wait_ge(s_ld_ev, 32)
                nb, seq = NBATCH[a], batches(a)
                with act.Fori(0, 4) as i:
                    P = 4 * a + i
                    act.wait_ge(s_w_used, base + 3 * i + 1)
                    for h in range(2):
                        lo, src = 64 * h, 0
                        col = bias[lo:lo + 64, bass.ds(b0 + i, 1)]
                        for half in (h, 1 - h):
                            ins = act.activation(flat(k_hi[64 * half:64 * half + 64, h, :]),
                                                 ps[lo:lo + 64, 0:3, 0:NP], ACT.Identity, bias=col)
                    ins.then_inc(s_k_hi, 1)
                    act.wait_ge(s_w_used, base + 3 * i + 2)
                    for h in range(2):
                        lo = 64 * h
                        ins = act.activation(flat(q_stack[lo:lo + 64, h, :]), ps[lo:lo + 64, 3:6, 0:NP], ACT.Identity,
                                             bias=bias[lo:lo + 64, bass.ds(b0 + 4 + i, 1)])
                    ins.then_inc(s_q_hi, 1)

                    def exps(n):
                        act.wait_ge(s_rowmax, 20 * P + (n + 1))
                        if n >= PROBS:
                            last = max(m for m, (g, b) in enumerate(seq) if g == (n - PROBS) // 2)
                            act.wait_ge(s_pt, BASE_B[a] + nb * i + (last + 1))
                        for x, (b, nbk, first, w) in enumerate(runs_of(plan[n][1])):
                            o = probs[:, n % PROBS, first:first + nbk * w].rearrange("p (b n) -> p b n", b=nbk)
                            ins = act.activation(o, ps[0:TOK, b:b + nbk, 0:w], ACT.Exp, scale=SCALE,
                                                 bias=stats[:, n % PROBS, 2:3],
                                                 accum_out=stats[:, n % PROBS, 4 + x:5 + x])
                        ins.then_inc(s_exp, 1)

                    def half_out(g):
                        h = g // 5
                        last = max(m for m, (gg, b) in enumerate(seq) if gg == g)
                        act.wait_ge(s_pv, BASE_B[a] + nb * i + (last + 1))
                        if g >= 1:
                            act.wait_ge(s_o, 10 * P + g)
                        act.activation(o_half[64 * h:64 * h + 64, :], ps[64 * (1 - h):64 * (1 - h) + 64, 5, 0:2 * TOK],
                                       ACT.Copy).then_inc(s_o_half, 1)

                    exps(0)
                    act.wait_ge(s_w_used, base + 3 * i + 3)
                    act.activation(flat(v_feat[:, :]), wide(5), ACT.Identity,
                                   bias=bias[:, bass.ds(b0 + 8 + i, 1)]).then_inc(s_v, 1)
                    exps(1)
                    for b, (t0, nt) in enumerate(TB):
                        act.wait_ge(s_vtr, 3 * P + (b + 1))
                        src = ps[0:TOK, 6 + b % 2, 0:nt * 128].rearrange("p (t d) -> p t d", d=128)
                        for h in range(2):
                            ins = act.activation(v_tok[:, t0:t0 + nt, h, 64 * h:64 * h + 64],
                                                 src[:, :, 64 * h:64 * h + 64], ACT.Copy)
                        ins.then_inc(s_v_hi, 1)
                    exps(2)
                    m = 0
                    for g in range(NT):
                        for what, b in order(a, g):
                            if what == "s":
                                exps(b)
                            if what == "t":
                                act.wait_ge(s_pt, BASE_B[a] + nb * i + (m + 1))
                                if m >= PT:
                                    act.wait_ge(s_pv, BASE_B[a] + nb * i + (m - PT + 1))
                                act.activation(pt_hi[:, m % PT, :], ps[0:TOK, 6 + m % 2, 0:4 * TOK], ACT.Copy)\
                                    .then_inc(s_pt_hi, 1)
                                m += 1
                                if b == 0 and g >= 1:
                                    half_out(g - 1)
                    half_out(NT - 1)
                for j in range(FB):
                    act.wait_ge(s_o, 40 * (a + 1))
                    act.activation(xc_hi[:, j, :], feat[:, j, :], ACT.Copy).then_inc(s_xc_hi, 1)
                for j in range(FB):
                    if name == "sp":
                        act.wait_ge(s_xt_st, 32)
                        act.wait_ge(s_w_used, base + 12 + j + 1)
                        act.activation(flat(xb_hi[:, j, :]), wide(3 * (j % 2)), ACT.Identity,
                                       bias=sp_vecs[:, 12 + j:13 + j]).then_inc(s_pj_a, 1)
                    elif name == "tp":
                        act.wait_ge(s_pj_d, 4 + 3 * j + 2)
                        act.activation(xa_hi[:, j, :], proj_tmp[:, :], ACT.Copy).then_inc(s_pj_a, 1)
                    else:
                        act.wait_ge(s_w_used, base + 12 + j + 1)
                        act.wait_ge(s_xc_lo, 4 * (a + 1))
                        act.activation(flat(feat[:, j, :]), wide(3 * (j % 2)), ACT.Identity,
                                       bias=vecs[:, V_COUT + j:V_COUT + j + 1]).then_inc(s_pj_a, 1)

            ln_root(3)
            banks_to_feature(TR4, [(xa_hi, V_MW, V_MB)])
            act.wait_ge(s_zero, 1)
            for j in range(FB):
                act.activation(feat[:, j, :], feat[:, j, :], ACT.Identity, bias=vecs[:, V_M2 + j:V_M2 + j + 1])\
                    .then_inc(s_b2, 1)
            with act.Fori(0, MLPQ) as i:
                for r in range(4):
                    act.wait_ge(s_w_used, W_MLP + 8 * i + (r + 1))
                    if r >= 2:
                        act.wait_ge(s_hid, 4 * i + (r - 1))
                    act.activation(flat(mlp_tmp[:, r % 2, :]), wide(3 * (r % 2)), ACT.Gelu,
                                   bias=vecs[:, bass.ds(V_M1 + 4 * i + r, 1)]).then_inc(s_gelu, 1)
                act.wait_ge(s_hid, 4 * i + 4)

        @block.vector
        def _(dve):
            wide = lambda b: ps[:, b:b + 3, 0:NP]
            flat = lambda ap: ap.rearrange("p (a n) -> p a n", a=3)
            dve.memset(f32(xa_hi[:, :, NODES:TP]), 0.0)
            dve.memset(f32(xa_lo[:, :, NODES:TP]), 0.0)
            dve.memset(small[:, :], 0.0).then_inc(s_constv, 1)
            dve.wait_ge(s_const, 2)
            dve.tensor_copy(identb[:, :], ident[:, :]).then_inc(s_constv, 1)

            def norm(n, src, dst):
                for t in range(NT):
                    ins = dve.bn_stats(ln_stats[:, t, :], src[:, t, :])
                ins.then_inc(s_ln, 1)
                dve.wait_ge(s_ln, 8 * n + 1)
                for t in range(NT):
                    ins = dve.bn_aggr(ln_mv[:, t, :], ln_stats[:, t, :])
                ins.then_inc(s_ln, 1)
                dve.wait_ge(s_ln, 8 * n + 2)
                v, r, q, h = (ln_r[:, x, :] for x in range(4))
                dve.tensor_scalar(v, ln_mv[:, :, 1], EPS, None, ALU.add).then_inc(s_ln, 1)
                dve.wait_ge(s_ln_sqrt, n + 1)
                dve.reciprocal(q, r).then_inc(s_ln, 1)
                dve.wait_ge(s_ln, 8 * n + 4)
                dve.tensor_tensor(h, q, q, ALU.mult).then_inc(s_ln, 1)
                dve.wait_ge(s_ln, 8 * n + 5)
                dve.tensor_tensor(h, h, v, ALU.mult).then_inc(s_ln, 1)
                dve.wait_ge(s_ln, 8 * n + 6)
                dve.tensor_scalar(h, h, -0.5, 1.5, ALU.mult, ALU.add).then_inc(s_ln, 1)
                dve.wait_ge(s_ln, 8 * n + 7)
                dve.tensor_tensor(r, q, h, ALU.mult).then_inc(s_ln, 1)
                dve.wait_ge(s_ln, 8 * n + 8)
                for t in range(NT):
                    dve.tensor_scalar(dst[:, t, :], src[:, t, :], ln_mv[:, t, 0:1], ln_r[:, 1, t:t + 1],
                                      ALU.subtract, ALU.mult).then_inc(s_ln_done, 1)

            def banks_to_feature(base, targets):
                m = base
                for t0, nt in TB:
                    for f in range(FB):
                        dve.wait_ge(s_tr_act, m - GAP[base] + 1)
                        span = slice(t0 * TOK, (t0 + nt) * TOK)
                        src = ps[:, 6 + m % 2, 0:nt * TOK]
                        if targets[0][2] is None:
                            hi, lo = targets[0][:2]
                            dve.tensor_tensor(lo[:, f, span], src, f32(hi[:, f, span]), ALU.subtract).then_inc(s_tr_dve, 1)
                        else:
                            written = {TR2: 0, TR4: 24}[base] + len(targets) * (m - base)
                            if written:
                                dve.wait_ge(s_tmp, written)
                            for x, (hi, lo, sc, bi) in enumerate(targets):
                                ins = dve.tensor_scalar(norm_tmp[:, x, 0:nt * TOK], src, vecs[:, sc + f:sc + f + 1],
                                                        vecs[:, bi + f:bi + f + 1], ALU.mult, ALU.add)
                            ins.then_inc(s_tr_dve, 1)
                            dve.wait_ge(s_tr_dve, m - GAP[base] + 1)
                            for x, (hi, lo, sc, bi) in enumerate(targets):
                                ins = dve.tensor_tensor(lo[:, f, span], norm_tmp[:, x, 0:nt * TOK], f32(hi[:, f, span]),
                                                        ALU.subtract)
                                ins.then_inc(s_tmp, 1)
                        m += 1

            dve.wait_ge(s_ld_x, 16)
            norm(0, tok_a, tok_a)
            banks_to_feature(0, [(xa_hi, xa_lo, None, None)])

            done = [0]

            def step(ins):
                done[0] += 1
                ins.then_inc(s_edge, 1)
                dve.wait_ge(s_edge, done[0])

            dve.wait_ge(s_ld_edge, 32)
            dve.wait_ge(s_const, 8)
            step(dve.tensor_copy(src_f[:, :], src_i[:, :]))
            step(dve.tensor_copy(dst_f[:, :], dst_i[:, :]))
            step(dve.tensor_scalar(src_tile[:, :], src_f[:, :], -(TOK - 1) / 2, 1.0 / TOK, ALU.add, ALU.mult))
            step(dve.tensor_scalar(src_tile[:, :], src_tile[:, :], MAGIC, -MAGIC, ALU.add, ALU.add))
            step(dve.tensor_scalar(dst_win[:, :], dst_f[:, :], -(WIN - 1) / 2, 1.0 / WIN, ALU.add, ALU.mult))
            step(dve.tensor_scalar(dst_win[:, :], dst_win[:, :], MAGIC, -MAGIC, ALU.add, ALU.add))
            step(dve.scalar_tensor_tensor(src_low[:, :], src_tile[:, :], -float(TOK), src_f[:, :], ALU.mult, ALU.add))
            step(dve.scalar_tensor_tensor(edge_key[:, :], src_tile[:, :], float(WIN), dst_f[:, :], ALU.mult, ALU.add))
            step(dve.scalar_tensor_tensor(edge_key[:, :], dst_win[:, :], float(WSHIFT - WIN), edge_key[:, :],
                                          ALU.mult, ALU.add))
            assert done[0] == EDGE_KEYS
            step(dve.tensor_reduce(chunk_f[0:NCH, 1:2], dst_win[:, :], AX.X, ALU.min))
            step(dve.tensor_reduce(chunk_f[0:NCH, 2:3], dst_win[:, :], AX.X, ALU.max))
            step(dve.tensor_copy(chunk_f[:, 0:1], chunk_i[:, :]))
            step(dve.tensor_scalar(chunk_f[:, 3:4], chunk_f[:, 0:1], -1001.0, None, ALU.add))
            step(dve.tensor_copy(iota_h[:, :], iota_i[:, :]))
            step(dve.tensor_copy(win_no[:, :], win_i[:, :]))
            step(dve.tensor_scalar(win_key[:, :], win_no[:, :], float(WSHIFT), None, ALU.mult))
            step(dve.tensor_scalar(inside[:, 0, :], win_no[0:NCH, :], chunk_f[0:NCH, 1:2], None, ALU.is_ge))
            step(dve.tensor_scalar(inside[:, 1, :], win_no[0:NCH, :], chunk_f[0:NCH, 2:3], None, ALU.is_le))
            step(dve.tensor_tensor(inside[:, 2, :], inside[:, 0, :], inside[:, 1, :], ALU.mult))
            step(dve.tensor_scalar(inside[:, 0, :], inside[:, 2, :], chunk_f[0:NCH, 3:4], 1000.0, ALU.mult, ALU.add))
            step(dve.tensor_scalar(inside[:, 1, :], inside[:, 2, :], chunk_f[0:NCH, 0:1], None, ALU.mult))
            assert done[0] == EDGE_INSIDE
            dve.wait_ge(s_edge_tr, 2)
            step(dve.tensor_copy(low_t[:, :, :], ps[0:ET, 0, 0:NCH * CH].rearrange("e (c p) -> e p c", c=CH)))
            step(dve.tensor_copy(key_t[:, :, :], ps[0:ET, 1, 0:NCH * CH].rearrange("e (c p) -> e p c", c=CH)))
            dve.wait_ge(s_edge_tr, 3)
            step(dve.tensor_reduce(bounds_c[:, 0:1], ps[0:NW, 2, 0:NCH], AX.X, ALU.min))
            step(dve.tensor_reduce(bounds_c[:, 1:2], ps[0:NW, 2, 128:128 + NCH], AX.X, ALU.max))
            assert done[0] == EDGE_BOUNDS
            dve.wait_ge(s_edge_tr, 4)
            step(dve.tensor_scalar(bounds_r[:, 0, :], ps[0:1, 3, 0:NW], float(NCH - 3), None, ALU.min))
            step(dve.scalar_tensor_tensor(bounds_r[:, 1, :], bounds_r[:, 0, :], 3.0, ps[0:1, 3, 64:64 + NW],
                                          ALU.add, ALU.max))
            done[0] += 1
            dve.tensor_copy(bounds_i[:, :], bounds_r[:, :, :].rearrange("o a w -> o (a w)")).then_inc(s_edge, 1)
            dve.wait_ge(s_edge, done[0])
            assert done[0] == EDGE_DONE
            dve.tensor_copy(small[:, 7:8], small[:, 5:6]).then_inc(s_hot_free, 2)

            count = dve.alloc_register("hot_count")
            dve.reg_mov(count, 0)

            def chunk_rows(w, p):
                n = dve.snap(count, min_val=0, max_val=NCH * NW)
                dve.wait_ge(s_hot_free, n + 1)
                for c in range(CH):
                    row = onehot[:, bass.ds((n % 2) * CH + c, 1), :].rearrange("p o n -> p (o n)")
                    low = low_t[:, bass.ds(p, 1), c:c + 1].rearrange("p o c -> p (o c)")
                    key = key_t[:, bass.ds(p, 1), c:c + 1].rearrange("p o c -> p (o c)")
                    dve.tensor_scalar(row[:, 0:ET], iota_h[0:ET, 0:ET], low, None, ALU.is_equal)
                    ins = dve.tensor_scalar(row[:, ET:ET + DH], iota_h[0:ET, :], win_key[0:ET, bass.ds(w, 1)], key,
                                            ALU.add, ALU.is_equal)
                ins.then_inc(s_hot, 1)
                dve.reg_add(count, count, 1)

            with dve.Fori(0, NW) as w:
                lo = dve.value_load(bounds_i[0:1, bass.ds(w, 1)], min_val=0, max_val=NCH - 3)
                hi = dve.value_load(bounds_i[0:1, bass.ds(w + NW, 1)], min_val=3, max_val=NCH)
                with dve.Fori(lo, hi) as p:
                    chunk_rows(w, p)

            dve.wait_ge(s_win_free, NW + 2)
            dve.tensor_reduce(deg_part[:, :], adj[:, :, :].rearrange("p t d -> p d t"), AX.X, ALU.add)\
                .then_inc(s_agg_dve, 1)
            dve.wait_ge(s_agg, 2)
            dve.tensor_scalar(flat(agg_tmp[:, :]), wide(3), 1.0, None, ALU.max).then_inc(s_agg_dve, 1)
            dve.wait_ge(s_agg_dve, 2)
            dve.reciprocal(inv_deg[:, :], agg_tmp[:, :]).then_inc(s_agg_dve, 1)
            for f in range(FB):
                dve.wait_ge(s_agg, AGG_OF[f] + 1)
                dve.wait_ge(s_agg_dve, 3 + 2 * f)
                if f:
                    dve.wait_ge(s_agg_act, f)
                dve.tensor_tensor(flat(agg_tmp[:, :]), wide(AGG_BANK[f]), flat(inv_deg[:, :]), ALU.mult)\
                    .then_inc(s_agg_dve, 1)
                dve.wait_ge(s_agg_act, f + 1)
                dve.tensor_tensor(xb_lo[:, f, :], agg_tmp[:, :], f32(xb_hi[:, f, :]), ALU.subtract).then_inc(s_agg_dve, 1)

            dve.memset(context[:, :], 0.0)
            with dve.Fori(0, 4) as i:
                dve.wait_ge(s_mk, i + 1)
                dve.tensor_reduce(small[:, 0:1], mix_k[:, 0:NODES], AX.X, ALU.max, negate=True).then_inc(s_mmax, 1)
                dve.wait_ge(s_mexp, i + 1)
                dve.reciprocal(small[:, 2:3], small[:, 1:2]).then_inc(s_mrecip, 1)
                for b, (t0, nt) in enumerate(TB):
                    dve.wait_ge(s_mtr, 6 * i + (3 + b + 1))
                    dve.tensor_copy(mix_vt[:, t0:t0 + nt, :], ps[0:TOK, 6 + (b + 1) % 2, 0:nt * 128]
                                    .rearrange("p (t d) -> p t d", d=128)).then_inc(s_mv_out, 1)
                dve.wait_ge(s_ctx, i + 1)
                dve.wait_ge(s_mrecip, i + 1)
                for h in range(2):
                    s = slice(64 * h, 64 * h + 64)
                    ins = dve.tensor_scalar(context[s, s], ps[s, 3, s], small[s, 2:3], None, ALU.mult)
                ins.then_inc(s_ctx_out, 1)
                dve.wait_ge(s_mo_act, i + 1)
                one = lambda t: t[:, bass.ds(i, 1), :].rearrange("p o n -> p (o n)")
                dve.tensor_tensor(flat(one(xb_lo)), wide(0), flat(f32(one(xb_hi))), ALU.subtract).then_inc(s_mo_dve, 1)
            for j in range(FB):
                dve.wait_ge(s_w_used, W_MIXO + j + 1)
                dve.scalar_tensor_tensor(flat(feat[:, j, :]), wide(3 * (j % 2)), vecs[:, V_MIXO + j:V_MIXO + j + 1],
                                         flat(feat[:, j, :]), ALU.add, ALU.add).then_inc(s_mixout, 1)

            dve.wait_ge(s_x_again, 16)
            for t in range(NT):
                dve.wait_ge(s_tr, TR1 + t + 1)
                dve.tensor_tensor(tok_a[:, t, :], ps[0:TOK, 6 + t % 2, :], x_again[:, t, :], ALU.add).then_inc(s_x1, 1)
            dve.wait_ge(s_x1, NT)
            dve.memset(f32(xa_hi[:, :, NODES:TP]), 0.0)
            dve.memset(f32(xa_lo[:, :, NODES:TP]), 0.0)
            norm(1, tok_a, tok_b)
            dve.wait_ge(s_st, 16)
            dve.wait_ge(s_ln_done, 2 * NT)
            norm(2, tok_b, tok_a)

            dve.wait_ge(s_pool_mm, 1)
            dve.tensor_copy(pooled[:, :], ps[:, 5, 0:FB]).then_inc(s_route, 1)
            dve.wait_ge(s_pool_mm, 3)
            dve.wait_ge(s_ld_router, 48)
            dve.tensor_tensor(route[:, 0:8], ps[0:1, 5, 16:24], router_b2[:, :], ALU.add).then_inc(s_route, 1)
            dve.wait_ge(s_route, 2)
            dve.tensor_reduce(route[:, 8:9], route[:, 0:8], AX.X, ALU.max, negate=True).then_inc(s_route, 1)
            dve.wait_ge(s_route_act, 2)
            dve.reciprocal(route[:, 10:11], route[:, 9:10]).then_inc(s_route, 1)
            dve.wait_ge(s_route, 4)
            dve.tensor_scalar(route[:, 24:32], route[:, 16:24], route[:, 10:11], None, ALU.mult).then_inc(s_route, 1)
            dve.wait_ge(s_route, 5)
            dve.tensor_reduce(route[:, 32:34], route[:, 24:32].rearrange("o (a n) -> o a n", a=2), AX.X, ALU.max)\
                .then_inc(s_route, 1)
            dve.wait_ge(s_route, 6)
            dve.wait_ge(s_const, 11)
            for h in range(2):
                ins = dve.tensor_scalar(route[:, 40 + 4 * h:44 + 4 * h], route[:, 24 + 4 * h:28 + 4 * h],
                                        route[:, 32 + h:33 + h], None, ALU.is_ge)
            dve.tensor_copy(expert_no[:, :], expert_no_i[:, :]).then_inc(s_route, 1)
            dve.wait_ge(s_route, 7)
            dve.tensor_tensor(route[:, 48:56], route[:, 40:48], expert_no[:, :], ALU.mult).then_inc(s_route, 1)
            dve.wait_ge(s_route, 8)
            dve.tensor_reduce(route[:, 56:58], route[:, 48:56].rearrange("o (a n) -> o a n", a=2), AX.X, ALU.min)\
                .then_inc(s_route, 1)
            dve.wait_ge(s_route, 9)
            dve.tensor_scalar(route_i[:, :], route[:, 56:58], 100.0, None, ALU.add).then_inc(s_route, 1)
            banks_to_feature(TR2, [(xa_hi, xa_lo, V_SW, V_SB), (xb_hi, xb_lo, V_TW, V_TB)])

            for a, (name, base, causal) in enumerate(ATT):
                plan = score_plan(causal)
                bias, b0 = {"sp": (sp_vecs, 0), "tp": (tp_vecs, 0), "cr": (vecs, V_CIN)}[name]
                if a == 0:
                    dve.wait_ge(s_ld_ev, 32)
                nb = NBATCH[a]
                with dve.Fori(0, 4) as i:
                    P = 4 * a + i
                    dve.wait_ge(s_k_hi, P + 1)
                    for h in range(2):
                        s = slice(64 * h, 64 * h + 64)
                        ins = dve.scalar_tensor_tensor(flat(k_lo[s, h, :]), ps[s, 0:3, 0:NP],
                                                       bias[s, bass.ds(b0 + i, 1)], flat(f32(k_hi[s, h, :])),
                                                       ALU.add, ALU.subtract)
                    ins.then_inc(s_k_half, 1)
                    dve.wait_ge(s_k_half, P + 1)
                    for h in range(2):
                        s, o = slice(64 * h, 64 * h + 64), slice(64 * (1 - h), 64 * (1 - h) + 64)
                        ins = dve.tensor_copy(k_lo[o, h, :], f32(k_lo[s, h, :]))
                    ins.then_inc(s_k_lo, 1)
                    dve.wait_ge(s_q_hi, P + 1)
                    for h in range(2):
                        s, o = slice(64 * h, 64 * h + 64), slice(64 * (1 - h), 64 * (1 - h) + 64)
                        ins = dve.scalar_tensor_tensor(flat(q_stack[o, h, :]), ps[s, 3:6, 0:NP],
                                                       bias[s, bass.ds(b0 + 4 + i, 1)], flat(f32(q_stack[s, h, :])),
                                                       ALU.add, ALU.subtract)
                    ins.then_inc(s_q_lo, 1)

                    def shift(n):
                        st = stats[:, n % PROBS, :]
                        runs = runs_of(plan[n][1])
                        dve.wait_ge(s_score, 20 * P + (n + 1))
                        for x, (b, nbk, first, w) in enumerate(runs):
                            ins = dve.tensor_reduce(st[:, x:x + 1], ps[0:TOK, b:b + nbk, 0:w], AX.XY, ALU.max, negate=True)
                        ins.then_inc(s_mx, 1)
                        dve.wait_ge(s_mx, 20 * P + (n + 1))
                        if len(runs) > 1:
                            ins = dve.tensor_scalar(st[:, 2:3], st[:, 0:1], st[:, 1:2], SCALE, ALU.min, ALU.mult)
                        else:
                            ins = dve.tensor_scalar(st[:, 2:3], st[:, 0:1], SCALE, None, ALU.mult)
                        ins.then_inc(s_rowmax, 1)

                    def recip(n):
                        st = stats[:, n % PROBS, :]
                        dve.wait_ge(s_exp, 20 * P + (n + 1))
                        if len(runs_of(plan[n][1])) > 1:
                            ins = dve.tensor_tensor(st[:, 6:7], st[:, 4:5], st[:, 5:6], ALU.add)
                        else:
                            ins = dve.tensor_copy(st[:, 6:7], st[:, 4:5])
                        ins.then_inc(s_sum, 1)
                        dve.wait_ge(s_sum, 20 * P + (n + 1))
                        dve.reciprocal(st[:, 7:8], st[:, 6:7]).then_inc(s_recip, 1)

                    def out_tiles(g):
                        s = slice(64 * (g // 5), 64 * (g // 5) + 64)
                        dve.wait_ge(s_o_half, 10 * P + (g + 1))
                        o = feat[s, bass.ds(i, 1), 2 * TOK * (g % 5):2 * TOK * (g % 5 + 1)].rearrange("p o n -> p (o n)")
                        dve.tensor_tensor(o, ps[s, 5, 0:2 * TOK], o_half[s, :], ALU.add).then_inc(s_o, 1)

                    shift(0)
                    recip(0)
                    shift(1)
                    for b, (t0, nt) in enumerate(TB):
                        dve.wait_ge(s_v_hi, 3 * P + (b + 1))
                        src = ps[0:TOK, 6 + b % 2, 0:nt * 128].rearrange("p (t d) -> p t d", d=128)
                        for h in range(2):
                            s, o = slice(64 * h, 64 * h + 64), slice(64 * (1 - h), 64 * (1 - h) + 64)
                            ins = dve.tensor_tensor(v_tok[:, t0:t0 + nt, h, o], src[:, :, s],
                                                    f32(v_tok[:, t0:t0 + nt, h, s]), ALU.subtract)
                        ins.then_inc(s_v_lo, 1)
                    recip(1)
                    shift(2)
                    m, late = 0, [2]
                    for g in range(NT):
                        for what, b in order(a, g):
                            if what == "s":
                                while late:
                                    recip(late.pop(0))
                                shift(b)
                                late.append(b)
                            if what == "t":
                                dve.wait_ge(s_pt_hi, BASE_B[a] + nb * i + (m + 1))
                                if m >= PT:
                                    dve.wait_ge(s_pv, BASE_B[a] + nb * i + (m - PT + 1))
                                dve.tensor_tensor(pt_lo[:, m % PT, :], ps[0:TOK, 6 + m % 2, 0:4 * TOK],
                                                  f32(pt_hi[:, m % PT, :]), ALU.subtract).then_inc(s_pt_lo, 1)
                                m += 1
                                if b == 0 and g >= 1:
                                    out_tiles(g - 1)
                        while late and late[0] <= 2 * g + 3:
                            recip(late.pop(0))
                    out_tiles(NT - 1)
                for j in range(FB):
                    dve.wait_ge(s_xc_hi, 4 * a + j + 1)
                    dve.tensor_tensor(xc_lo[:, j, :], feat[:, j, :], f32(xc_hi[:, j, :]), ALU.subtract)\
                        .then_inc(s_xc_lo, 1)
                for j in range(FB):
                    bank = wide(3 * (j % 2))
                    if name == "sp":
                        dve.wait_ge(s_pj_a, j + 1)
                        dve.scalar_tensor_tensor(flat(xb_lo[:, j, :]), bank, sp_vecs[:, 12 + j:13 + j],
                                                 flat(f32(xb_hi[:, j, :])), ALU.add, ALU.subtract).then_inc(s_pj_d, 1)
                    if name == "tp":
                        dve.wait_ge(s_w_used, base + 12 + j + 1)
                        if j:
                            dve.wait_ge(s_pj_d, 4 + 3 * j)
                        dve.scalar_tensor_tensor(flat(proj_tmp[:, :]), bank, tp_vecs[:, 12 + j:13 + j],
                                                 flat(f32(xa_hi[:, j, :])), ALU.add, ALU.add).then_inc(s_pj_d, 1)
                        dve.wait_ge(s_pj_d, 4 + 3 * j + 1)
                        dve.tensor_tensor(proj_tmp[:, :], proj_tmp[:, :], f32(xa_lo[:, j, :]), ALU.add).then_inc(s_pj_d, 1)
                        dve.wait_ge(s_pj_a, 4 + j + 1)
                        dve.tensor_tensor(xa_lo[:, j, :], proj_tmp[:, :], f32(xa_hi[:, j, :]), ALU.subtract)\
                            .then_inc(s_pj_d, 1)

            dve.wait_ge(s_xn_back, 16)
            for t in range(NT):
                dve.wait_ge(s_tr, TR3 + t + 1)
                dve.tensor_tensor(tok_a[:, t, :], ps[0:TOK, 6 + t % 2, :], tok_b[:, t, :], ALU.add).then_inc(s_x1, 1)
            dve.memset(feat[:, :, :], 0.0).then_inc(s_zero, 1)
            dve.wait_ge(s_x1, 2 * NT)
            norm(3, tok_a, tok_b)
            banks_to_feature(TR4, [(xa_hi, xa_lo, V_MW, V_MB)])
            dve.wait_ge(s_b2, FB)
            with dve.Fori(0, MLPQ) as i:
                for r in range(4):
                    dve.wait_ge(s_gelu, 4 * i + (r + 1))
                    dve.tensor_copy(xb_hi[:, r, :], mlp_tmp[:, r % 2, :]).then_inc(s_hid_hi, 1)
                    dve.wait_ge(s_hid_hi, 4 * i + (r + 1))
                    dve.tensor_tensor(xb_lo[:, r, :], mlp_tmp[:, r % 2, :], f32(xb_hi[:, r, :]), ALU.subtract)\
                        .then_inc(s_hid, 1)
                for r in range(4):
                    dve.wait_ge(s_w_used, W_MLP + 8 * i + (4 + r + 1))
                    f = flat(feat[:, r, :])
                    dve.tensor_tensor(f, wide(3 * (r % 2)), f, ALU.add).then_inc(s_acc, 1)
            dve.wait_ge(s_x1_back, 16)
            for t in range(NT):
                dve.wait_ge(s_tr, TR5 + t + 1)
                dve.tensor_tensor(tok_a[:, t, :], ps[0:TOK, 6 + t % 2, :], tok_a[:, t, :], ALU.add).then_inc(s_sum2, 1)
                dve.wait_ge(s_sum2, t + 1)
                dve.tensor_tensor(tok_b[:, t, :], tok_a[:, t, :], tok_b[:, t, :], ALU.add).then_inc(s_final, 1)

        @block.tensor
        def _(pe):
            def linear(k, slot, x_hi, x_lo, bank, first=True, last=True):
                pe.wait_ge(s_w_split, k + 1)
                parts = ((w_hi, x_hi), (w_hi, x_lo), (w_lo, x_hi))
                for c in range(FB):
                    for n, (w, x) in enumerate(parts):
                        for p in range(3):
                            ins = pe.matmul(ps[:, bank + p, 0:NP], w[:, slot, 128 * c:128 * c + 128],
                                            x[:, c, NP * p:NP * p + NP], start=(first and c == 0 and n == 0),
                                            stop=(last and c == FB - 1 and n == 2))
                ins.then_inc(s_w_used, 1)

            def to_feature(base, norm_no, src):
                m = base
                for t0, nt in TB:
                    pe.wait_ge(s_ln_done, NT * norm_no + t0 + nt)
                    for f in range(FB):
                        if m - base >= 2:
                            pe.wait_ge(s_tr_dve, TRD[base] + (m - base) - 1)
                        for t in range(nt):
                            ins = pe.transpose(ps[:, 6 + m % 2, t * TOK:(t + 1) * TOK],
                                               src[:, t0 + t, 128 * f:128 * f + 128], ident[0:TOK, 0:TOK])
                        ins.then_inc(s_tr, 1)
                        m += 1

            def to_nodes(base, readers, read_base):
                for t in range(NT):
                    if t >= 2:
                        pe.wait_ge(readers, read_base + t - 1)
                    for f in range(FB):
                        ins = pe.transpose(ps[0:TOK, 6 + t % 2, 128 * f:128 * f + 128],
                                           feat[:, f, t * TOK:(t + 1) * TOK], ident[:, :])
                    ins.then_inc(s_tr, 1)

            pe.wait_ge(s_constv, 2)
            to_feature(0, 0, tok_a)

            pe.wait_ge(s_edge, EDGE_KEYS)
            for x, src in enumerate((src_low, edge_key)):
                for c in range(CH):
                    ins = pe.transpose(ps[0:ET, x, c * NCH:(c + 1) * NCH], src[:, c * ET:(c + 1) * ET], ident[0:NCH, 0:NCH])
                ins.then_inc(s_edge_tr, 1)
            pe.wait_ge(s_edge, EDGE_INSIDE)
            for x in range(2):
                ins = pe.transpose(ps[0:NW, 2, 128 * x:128 * x + NCH], inside[:, x, :], ident[0:NCH, 0:NCH])
            ins.then_inc(s_edge_tr, 1)
            pe.wait_ge(s_edge, EDGE_BOUNDS)
            for x in range(2):
                ins = pe.transpose(ps[0:1, 3, 64 * x:64 * x + NW], bounds_c[:, x:x + 1], ident[0:NW, 0:NW])
            ins.then_inc(s_edge_tr, 1)
            pe.wait_ge(s_edge, EDGE_DONE)

            count = pe.alloc_register("hot_used")
            pe.reg_mov(count, 0)

            def chunk_counts(bank, first, last):
                n = pe.snap(count, min_val=0, max_val=NCH * NW)
                pe.wait_ge(s_hot, n + 1)
                for c in range(CH):
                    row = onehot[:, bass.ds((n % 2) * CH + c, 1), :].rearrange("p o n -> p (o n)")
                    ins = pe.matmul(ps[0:ET, bank, 0:DH], row[:, 0:ET], row[:, ET:ET + DH],
                                    start=(first and c == 0), stop=(last and c == CH - 1), skip_group_check=True)
                ins.then_inc(s_hot_free, 1)
                if last:
                    pe.matmul(ps[0:1, 4, 0:1], identb[:, 0:1], identb[:, 0:1], start=True, stop=True).then_inc(s_win, 1)
                pe.reg_add(count, count, 1)

            with pe.Fori(0, NW // 2) as w2:
                for par in range(2):
                    w = 2 * w2 + par
                    lo = pe.value_load(bounds_i[0:1, bass.ds(w, 1)], min_val=0, max_val=NCH - 3)
                    hi = pe.value_load(bounds_i[0:1, bass.ds(w + NW, 1)], min_val=3, max_val=NCH)
                    pe.wait_ge(s_win_free, w + 1)
                    chunk_counts(par, True, False)
                    with pe.Fori(lo + 1, hi - 1):
                        chunk_counts(par, False, False)
                    chunk_counts(par, False, True)

            pe.wait_ge(s_win_free, NW + 2)

            def aggregate(f, bank):
                for t in range(NT):
                    for p in range(3):
                        ins = pe.matmul(ps[:, bank + p, 0:NP], tok_a[:, t, 128 * f:128 * f + 128],
                                        adj[:, t, NP * p:NP * p + NP], start=(t == 0), stop=(t == NT - 1))
                ins.then_inc(s_agg, 1)

            aggregate(0, 0)
            pe.wait_ge(s_agg_dve, 1)
            for p in range(3):
                ins = pe.matmul(ps[:, 3 + p, 0:NP], ones[0:TOK, :], deg_part[:, NP * p:NP * p + NP], start=True, stop=True)
            ins.then_inc(s_agg, 1)
            pe.wait_ge(s_agg_dve, 4)
            aggregate(1, 0)
            aggregate(2, 3)
            pe.wait_ge(s_agg_dve, 6)
            aggregate(3, 0)

            for j in range(FB):
                if j >= 2:
                    pe.wait_ge(s_gnn, j - 1)
                if j == 0:
                    pe.wait_ge(s_agg_dve, 11)
                    pe.wait_ge(s_tr_dve, 12)
                linear(W_GNN + 2 * j, SLOTS[2 * j], xa_hi, xa_lo, 3 * (j % 2), last=False)
                linear(W_GNN + 2 * j + 1, SLOTS[2 * j + 1], xb_hi, xb_lo, 3 * (j % 2), first=False)

            pe.wait_ge(s_gnn, 4)
            with pe.Fori(0, 4) as i:
                linear(W_MIX + 3 * i, 0, xa_hi, xa_lo, 0)
                linear(W_MIX + 3 * i + 1, 1, xa_hi, xa_lo, 3)
                pe.wait_ge(s_mk, i + 1)
                linear(W_MIX + 3 * i + 2, 2, xa_hi, xa_lo, 0)
                for m in range(6):
                    src, (t0, nt) = (mix_k if m < 3 else mix_v), TB[m % 3]
                    if m == 0:
                        pe.wait_ge(s_mexp, i + 1)
                    if m == 3:
                        pe.wait_ge(s_mv, i + 1)
                    if 2 <= m < 5:
                        pe.wait_ge(s_mk_out, 3 * i + (m - 1))
                    if m == 5:
                        pe.wait_ge(s_mv_out, 3 * i + 1)
                    for t in range(nt):
                        ins = pe.transpose(ps[0:TOK, 6 + m % 2, 128 * t:128 * t + 128],
                                           src[:, (t0 + t) * TOK:(t0 + t + 1) * TOK], ident[:, :])
                    ins.then_inc(s_mtr, 1)
                pe.wait_ge(s_mv_out, 3 * i + 3)
                pe.wait_ge(s_mq, i + 1)
                for t in range(NT):
                    ins = pe.matmul(ps[:, 3, 0:128], mix_kt[:, t, :], mix_vt[:, t, :], start=(t == 0), stop=(t == NT - 1))
                ins.then_inc(s_ctx, 1)
                pe.wait_ge(s_ctx_out, i + 1)
                for p in range(3):
                    ins = pe.matmul(ps[:, p, 0:NP], context[:, :], mix_q[:, NP * p:NP * p + NP], start=True, stop=True)
                ins.then_inc(s_mo, 1)
                pe.wait_ge(s_mo_dve, i + 1)
            for j in range(FB):
                if j >= 2:
                    pe.wait_ge(s_mixout, j - 1)
                linear(W_MIXO + j, SLOTS[W_MIXO + j], xb_hi, xb_lo, 3 * (j % 2))
            pe.wait_ge(s_mixout, 4)
            to_nodes(TR1, s_x1, 0)

            pe.wait_ge(s_ln_done, 2 * NT)
            pe.wait_ge(s_const, 11)
            for f in range(FB):
                for t in range(NT):
                    ins = pe.matmul(ps[:, 5, f:f + 1], tok_b[:, t, 128 * f:128 * f + 128], mean_col[:, :],
                                    start=(t == 0), stop=(t == NT - 1))
            ins.then_inc(s_pool_mm, 1)
            pe.wait_ge(s_route, 1)
            pe.wait_ge(s_ld_router, 48)
            for f in range(FB):
                ins = pe.matmul(ps[:, 5, 8:9], router_w1[:, f, :], pooled[:, f:f + 1], start=(f == 0), stop=(f == FB - 1))
            ins.then_inc(s_pool_mm, 1)
            pe.wait_ge(s_route_act, 1)
            pe.matmul(ps[0:1, 5, 16:24], small[:, 4:5], router_w2[:, :], start=True, stop=True).then_inc(s_pool_mm, 1)
            to_feature(TR2, 2, tok_a)

            for a, (name, base, causal) in enumerate(ATT):
                plan = score_plan(causal)
                q_hi_src, q_lo_src = (xb_hi, xb_lo) if name == "cr" else (xa_hi, xa_lo)
                nb, seq = NBATCH[a], batches(a)
                if name == "sp":
                    pe.wait_ge(s_tmp, 24)
                if name == "tp":
                    pe.wait_ge(s_xt_ld, 32)
                    pe.wait_ge(s_pj_d, 4)
                if name == "cr":
                    pe.wait_ge(s_pj_d, 16)
                with pe.Fori(0, 4) as i:
                    P = 4 * a + i
                    linear(base + 3 * i, 0, xa_hi, xa_lo, 0)
                    linear(base + 3 * i + 1, 1, q_hi_src, q_lo_src, 3)

                    def scores(n):
                        h, t = n // NT, n % NT
                        for j, (b, first, w) in enumerate(plan[n][1]):
                            users = [x for x in range(n) if any(bb == b for bb, _, _ in plan[x][1])]
                            if users:
                                pe.wait_ge(s_exp, 20 * P + (users[-1] + 1))
                            masked = causal and j == len(plan[n][1]) - 1
                            query = q_stack[:, h, t * TOK:(t + 1) * TOK]
                            pe.matmul(ps[0:TOK, b, 0:w], query, k_hi[:, h, first:first + w], start=True, stop=False)
                            if masked:
                                off = TOK * (1 - t % 2)
                                pe.matmul(ps[0:TOK, b, w - 2 * TOK:w], identb[0:TOK, 0:TOK],
                                          causal_mask[:, off:off + 2 * TOK], start=False, stop=False,
                                          skip_group_check=True)
                            ins = pe.matmul(ps[0:TOK, b, 0:w], query, k_lo[:, h, first:first + w], start=False, stop=True)
                        ins.then_inc(s_score, 1)

                    pe.wait_ge(s_k_lo, P + 1)
                    pe.wait_ge(s_q_lo, P + 1)
                    scores(0)
                    linear(base + 3 * i + 2, 2, xa_hi, xa_lo, 5)
                    scores(1)
                    for b, (t0, nt) in enumerate(TB):
                        pe.wait_ge(s_v, P + 1)
                        if b == 2:
                            pe.wait_ge(s_v_lo, 3 * P + 1)
                        for t in range(nt):
                            ins = pe.transpose(ps[0:TOK, 6 + b % 2, 128 * t:128 * t + 128],
                                               v_feat[:, (t0 + t) * TOK:(t0 + t + 1) * TOK], ident[:, :])
                        ins.then_inc(s_vtr, 1)
                    scores(2)
                    pe.wait_ge(s_v_lo, 3 * P + 3)
                    m = 0
                    done = 0
                    for g in range(NT):
                        h = g // 5
                        kts = 2 * len([1 for gg, _ in seq if gg == g])
                        for what, b in order(a, g):
                            if what == "s":
                                scores(b)
                            if what == "t":
                                if b == 0:
                                    pe.wait_ge(s_prob, 20 * P + (2 * g + 2))
                                if m >= 2:
                                    pe.wait_ge(s_pt_lo, BASE_B[a] + nb * i + (m - 1))
                                for x in range(4):
                                    kt, n = 2 * b + x // 2, 2 * g + x % 2
                                    ins = pe.transpose(ps[0:TOK, 6 + m % 2, x * TOK:(x + 1) * TOK],
                                                       probs[:, n % PROBS, kt * TOK:(kt + 1) * TOK], ident[0:TOK, 0:TOK])
                                ins.then_inc(s_pt, 1)
                                m += 1
                            if what == "p":
                                pe.wait_ge(s_pt_lo, BASE_B[a] + nb * i + (done + 1))
                                if b == 0 and g >= 1:
                                    pe.wait_ge(s_o, 10 * P + g)
                                for x in range(2):
                                    kt = 2 * b + x
                                    for part in (pt_hi, pt_lo):
                                        ins = pe.matmul(ps[:, 5, 0:2 * TOK], v_tok[:, kt, h, :],
                                                        part[:, done % PT, 2 * TOK * x:2 * TOK * (x + 1)],
                                                        start=(kt == 0 and part is pt_hi),
                                                        stop=(kt == kts - 1 and part is pt_lo))
                                ins.then_inc(s_pv, 1)
                                done += 1
                    pe.wait_ge(s_o, 10 * P + 10)
                pe.wait_ge(s_xc_lo, 4 * (a + 1))
                for j in range(FB):
                    if j >= 2:
                        if name == "sp":
                            pe.wait_ge(s_pj_d, j - 1)
                        elif name == "tp":
                            pe.wait_ge(s_pj_d, 4 + 3 * (j - 2) + 1)
                        else:
                            pe.wait_ge(s_pj_a, 8 + j - 1)
                    linear(base + 12 + j, SLOTS[base + 12 + j], xc_hi, xc_lo, 3 * (j % 2))

            pe.wait_ge(s_pj_a, 12)
            to_nodes(TR3, s_x1, NT)
            to_feature(TR4, 3, tok_b)
            pe.wait_ge(s_tmp, 36)
            with pe.Fori(0, MLPQ) as i:
                for r in range(4):
                    if r >= 2:
                        pe.wait_ge(s_gelu, 4 * i + (r - 1))
                    linear(W_MLP + 8 * i + r, r % 3, xa_hi, xa_lo, 3 * (r % 2))
                for r in range(4):
                    if r < 2:
                        pe.wait_ge(s_gelu, 4 * i + (r + 3))
                    else:
                        pe.wait_ge(s_acc, 4 * i + (r - 1))
                    if r == 0:
                        pe.wait_ge(s_hid, 4 * i + 4)
                    linear(W_MLP + 8 * i + 4 + r, (4 + r) % 3, xb_hi, xb_lo, 3 * (r % 2))
                pe.wait_ge(s_acc, 4 * i + 4)
            to_nodes(TR5, s_sum2, 0)


def kernel(**inputs):
    import concourse.bacc as bacc
    from concourse.bass_utils import run_bass_kernel_spmd

    g = {k: np.asarray(v) for k, v in inputs.items()}

    def blocks(w):
        o, n = w.shape[-2:]
        w = w.reshape(-1, o // 128, 128, n // 512, 4, 128)
        return w.transpose(0, 1, 3, 5, 4, 2)

    def flat(b):
        return np.ascontiguousarray(b).reshape(-1, 128, BLK)

    def columns(v):
        return np.swapaxes(v.reshape(v.shape[:-1] + (-1, 128)), -1, -2)

    def kqv(w):
        q, k, v = np.split(w, 3, axis=-2)
        return np.concatenate([k, q, v], axis=-2)

    def kqv_b(v):
        q, k, w = np.split(v, 3, axis=-1)
        return np.concatenate([k, q, w], axis=-1)

    p = "L0_ffn_"
    w1 = blocks(g[p + "mlp_w1"])[0, :, 0].reshape(MLPQ, 4, 128, 4, 128)
    w2 = blocks(g[p + "mlp_w2"])[0].transpose(1, 0, 2, 3, 4)
    experts = lambda qkv, o: np.ascontiguousarray(np.concatenate([qkv, o], axis=1)).reshape(-1, 128, BLK)
    e4 = lambda w: blocks(w).reshape(EXPERTS, -1, 128, BLK)
    arrays = {
        "x": np.ascontiguousarray(g["x"]),
        "src": np.ascontiguousarray(g["src"]),
        "dst": np.ascontiguousarray(g["dst"]),
        "w_gnn": flat(np.stack([blocks(g["L0_gnn_W_self"])[0, :, 0], blocks(g["L0_gnn_W_neigh"])[0, :, 0]], axis=1)),
        "w_mix": flat(blocks(np.concatenate([kqv(g["L0_mix_W_qkv"]), g["L0_mix_W_out"]]))),
        "w_sp": experts(e4(kqv(g[p + "sp_in_w"])), e4(g[p + "sp_out_w"])),
        "w_tp": experts(e4(np.concatenate([g[p + "tk_w"], g[p + "tq_w"], g[p + "tv_w"]], axis=1)), e4(g[p + "tp_w"])),
        "w_cr": flat(blocks(np.concatenate([kqv(g[p + "cross_in_w"]), g[p + "cross_out_w"]]))),
        "w_mlp": flat(np.concatenate([w1, w2], axis=1)),
        "vecs": np.ascontiguousarray(np.concatenate([columns(v) for v in (
            g["L0_gnn_b"], kqv_b(g["L0_mix_b_qkv"]), g["L0_mix_b_out"], g[p + "norm_s_w"], g[p + "norm_s_b"],
            g[p + "norm_t_w"], g[p + "norm_t_b"], kqv_b(g[p + "cross_in_b"]), g[p + "cross_out_b"],
            g[p + "norm_mlp_w"], g[p + "norm_mlp_b"], g[p + "mlp_b1"], g[p + "mlp_b2"], g[p + "router_b1"])], axis=1)),
        "v_sp": np.ascontiguousarray(np.concatenate([columns(kqv_b(g[p + "sp_in_b"])), columns(g[p + "sp_out_b"])], axis=2)),
        "v_tp": np.ascontiguousarray(np.concatenate([columns(g[p + n]) for n in ("tk_b", "tq_b", "tv_b", "tp_b")], axis=2)),
        "router_w1": np.ascontiguousarray(g[p + "router_w1"].T.reshape(FB, 128, 128).transpose(1, 0, 2)),
        "router_w2": np.ascontiguousarray(g[p + "router_w2"].T),
        "router_b2": np.ascontiguousarray(g[p + "router_b2"].reshape(1, -1)),
    }
    nc = bacc.Bacc("TRN2", target_bir_lowering=False, num_devices=1)
    aps = {n: nc.dram_tensor("in_" + n, a.shape, mybir.dt.from_np(a.dtype), kind="ExternalInput").ap()
           for n, a in arrays.items()}
    out = nc.dram_tensor("out", [NODES, D], F32, kind="ExternalOutput").ap()
    build(nc, aps, out)
    r = run_bass_kernel_spmd(nc, [{"in_" + n: a for n, a in arrays.items()}], core_ids=[0])
    return r.results[0]["out"]
```

```python
import numpy as np
from contextlib import ExitStack

import concourse.bass as bass
from concourse import mybir

F32 = mybir.dt.float32
F32R = mybir.dt.float32r
F16 = mybir.dt.float16
BF16 = mybir.dt.bfloat16
I32 = mybir.dt.int32
ACT = mybir.ActivationFunctionType
ALU = mybir.AluOpType
AX = mybir.AxisListType

NODES, D, HEADS, EXPERTS = 1250, 512, 8, 4
HD = D // HEADS
SCALE = HD ** -0.5
TOK = 125
NT = NODES // TOK
FB = D // 128
NP = 418
TP = 3 * NP
EDGES = 2 * 20000 + NODES
ET = 125
CH = 3
NCH = EDGES // (ET * CH)
EPC = ET * CH
WIN = 32
NW = 40
DH = NT * WIN
WSHIFT = 512
MAGIC = 12582912.0
NEG = -3.0e38
EPS = 1e-5
MLPQ = 4
BLK = FB * 128

V_GNN, V_MIX, V_MIXO = 0, 4, 16
V_SW, V_SB, V_TW, V_TB = 20, 24, 28, 32
V_CIN, V_COUT, V_MW, V_MB, V_M1, V_M2, V_R1 = 36, 48, 52, 56, 60, 76, 80
NVEC = 81


def slots_of(lengths):
    out = []
    for n in lengths:
        out += [r % 3 for r in range(n)]
    return out


STRETCH = [8] + [3] * 4 + [4] + ([3] * 4 + [4]) * 3 + [8] * 4
SLOTS = slots_of(STRETCH)


def since(k):
    for d in range(1, k + 1):
        if SLOTS[k - d] == SLOTS[k]:
            return d
    return None


def since_in_loop(base, length, passes, r):
    return min(since(base + length * i + r) for i in range(passes))


W_GNN, W_MIX, W_MIXO = 0, 8, 20
W_SP, W_TP, W_CR, W_MLP = 24, 40, 56, 72
assert len(SLOTS) == W_MLP + 32

PROBS, PT = 5, 4
ROUTE_STEPS = 10
EDGE_KEYS, EDGE_INSIDE, EDGE_BOUNDS, EDGE_DONE = 9, 21, 25, 28
AGG_OF, AGG_BANK = [0, 2, 3, 4], [0, 0, 3, 0]

RING = 4
OUT_BANK = 4
T_BANK, T_BANKS = 5, 3
AHEAD = 3


def score_plan(causal):
    plan, at = [], 1
    for n in range(2 * NT):
        g = (n % NT) // 2
        width = 2 * TOK * (g + 1) if causal else NODES
        count = -(-width // 512)
        banks = [(at + j) % RING for j in range(count)]
        if count == 3:
            odd = 2 if banks[2] == 0 else 0
            sizes = [418 if j == odd else 416 for j in range(3)]
        elif count == 2:
            sizes = [width // 2 // 2 * 2, width - width // 2 // 2 * 2]
        else:
            sizes = [width]
        first = [sum(sizes[:j]) for j in range(count)]
        pieces = list(zip(banks, first, sizes))
        plan.append((width, pieces))
        at = (at + count) % RING
    return plan


def runs_of(pieces):
    runs = []
    for bank, first, n in pieces:
        if runs and runs[-1][0] + runs[-1][1] == bank and runs[-1][3] == n:
            runs[-1][1] += 1
        else:
            runs.append([bank, 1, first, n])
    return runs



def build(nc, A, out):
    ctx = ExitStack()
    with ctx:
        def sem(name):
            return ctx.enter_context(nc.semaphore(name))

        place = {"end": -(-nc.sbuf_base // 64) * 64}

        def sb(name, shape, dt, pos=None):
            pos = place["end"] if pos is None else pos
            size = 2 if dt in (F16, BF16) else 4
            for s in shape[1:]:
                size *= s
            place["end"] = pos + -(-size // 64) * 64
            assert place["end"] <= nc.sbuf_usable_end, name
            return nc.alloc_sbuf_tensor_at(name, shape, dt, offset=pos)

        ident = sb("ident", [128, 128], F32)
        identb = sb("identb", [128, 128], BF16)
        causal_mask = sb("causal_mask", [TOK, 3 * TOK], BF16)
        vecs = sb("vecs", [128, NVEC], F32)
        sp_vecs = sb("sp_vecs", [128, 16], F32)
        tp_vecs = sb("tp_vecs", [128, 16], F32)
        small = sb("small", [128, 8], F32)
        pool_tick = sb("pool_tick", [128, 24], F32)
        w_raw = sb("w_raw", [128, 3, BLK], F32)
        w_hi = sb("w_hi", [128, 3, BLK], F32R)
        w_lo = sb("w_lo", [128, 3, BLK], F32R)
        xa_at = place["end"]
        xa_hi = sb("xa_hi", [128, FB, TP], F32R)
        xa_lo = sb("xa_lo", [128, FB, TP], F32R)
        xb_at = place["end"]
        xb_hi = sb("xb_hi", [128, FB, TP], F32R)
        xb_lo = sb("xb_lo", [128, FB, TP], F32R)
        feat_at = place["end"]
        feat = sb("feat", [128, FB, TP], F32)
        work_at = place["end"]

        tok_a = sb("tok_a", [TOK, NT, D], F32, work_at)
        tok_b_at = place["end"]
        adj = sb("adj", [TOK, NT, NW * WIN], F32)
        onehot = sb("onehot", [ET, 2 * CH, ET + DH], F16)
        src_i = sb("src_i", [NCH, EPC], I32, xb_at)
        dst_i = sb("dst_i", [NCH, EPC], I32)
        src_f = sb("src_f", [NCH, EPC], F32)
        dst_f = sb("dst_f", [NCH, EPC], F32)
        src_tile = sb("src_tile", [NCH, EPC], F32)
        src_low = sb("src_low", [NCH, EPC], F32)
        dst_win = sb("dst_win", [NCH, EPC], F32)
        edge_key = sb("edge_key", [NCH, EPC], F32)
        low_t = sb("low_t", [ET, NCH, CH], F32)
        key_t = sb("key_t", [ET, NCH, CH], F32)
        iota_i = sb("iota_i", [128, DH], I32)
        iota_h = sb("iota_h", [128, DH], F16)
        win_i = sb("win_i", [128, NW], I32)
        win_no = sb("win_no", [128, NW], F32)
        win_key = sb("win_key", [128, NW], F32)
        chunk_i = sb("chunk_i", [128, 1], I32)
        chunk_f = sb("chunk_f", [128, 4], F32)
        inside = sb("inside", [NCH, 3, NW], F32)
        bounds_c = sb("bounds_c", [NW, 2], F32)
        bounds_r = sb("bounds_r", [1, 2, NW], F32)
        bounds_i = sb("bounds_i", [1, 2 * NW], I32)
        assert place["end"] <= feat_at
        deg_part = sb("deg_part", [TOK, NW * WIN], F32, feat_at)
        inv_deg = sb("inv_deg", [128, TP], F32)
        agg_tmp = sb("agg_tmp", [128, TP], F32)
        ones = sb("ones", [128, 128], F32)
        assert place["end"] <= work_at

        mix_q = sb("mix_q", [128, TP], F32, work_at)
        mix_k = sb("mix_k", [128, TP], F32)
        mix_v = sb("mix_v", [128, TP], F32)
        mix_kt = sb("mix_kt", [TOK, NT, 128], F32)
        mix_vt = sb("mix_vt", [TOK, NT, 128], F32)
        context = sb("context", [128, 128], F32)

        x_again = sb("x_again", [TOK, NT, D], F32, xa_at)
        assert place["end"] <= xb_at
        tok_b = sb("tok_b", [TOK, NT, D], F32, tok_b_at)
        norm_tmp = sb("norm_tmp", [128, 2, 4 * TOK], F32)
        ln_stats = sb("ln_stats", [TOK, NT, 6], F32)
        ln_mv = sb("ln_mv", [TOK, NT, 2], F32)
        ln_r = sb("ln_r", [TOK, 4, NT], F32)
        router_w1 = sb("router_w1", [128, FB, 128], F32)
        router_w2 = sb("router_w2", [128, 2 * EXPERTS], F32)
        router_b2 = sb("router_b2", [1, 2 * EXPERTS], F32)
        mean_col = sb("mean_col", [TOK, 1], F32)
        pooled = sb("pooled", [128, FB], F32)
        route = sb("route", [1, 64], F32)
        expert_no = sb("expert_no", [1, 2 * EXPERTS], F32)
        expert_no_i = sb("expert_no_i", [1, 2 * EXPERTS], I32)
        route_i = sb("route_i", [1, 2], I32)
        mlp_tmp = sb("mlp_tmp", [128, 2, TP], F32)

        xc_hi = sb("xc_hi", [128, FB, TP], F32R, work_at)
        xc_lo = sb("xc_lo", [128, FB, TP], F32R)
        proj_tmp = sb("proj_tmp", [128, TP], F32)
        q_stack = sb("q_stack", [128, 2, TP], F32R, work_at)
        k_hi = sb("k_hi", [128, 2, TP], F32R)
        k_lo = sb("k_lo", [128, 2, TP], F32R)
        v_feat = sb("v_feat", [128, TP], F32)
        v_tok = sb("v_tok", [TOK, NT, 2, 128], F32R)
        probs = sb("probs", [TOK, PROBS, NODES], F32)
        pt_hi = sb("pt_hi", [TOK, PT, 4 * TOK], F32R)
        pt_lo = sb("pt_lo", [TOK, PT, 4 * TOK], F32R)
        o_half = sb("o_half", [128, 2 * TOK], F32)
        stats = sb("stats", [TOK, PROBS, 8], F32)

        ps = ctx.enter_context(nc.psum_tensor("ps", [128, 8, 512], F32))

        d_x1 = nc.dram_tensor("d_x1", [TOK, NT, D], F32, kind="Internal").ap()
        d_xn = nc.dram_tensor("d_xn", [TOK, NT, D], F32, kind="Internal").ap()
        d_xt = nc.dram_tensor("d_xt", [2, 128, FB, TP], F32, kind="Internal").ap()

        s_const = sem("s_const")
        s_constv = sem("s_constv")
        s_ld_x = sem("s_ld_x")
        s_ld_edge = sem("s_ld_edge")
        s_ld_vec = sem("s_ld_vec")
        s_ld_router = sem("s_ld_router")
        s_w_raw = [sem(f"s_w_raw{i}") for i in range(3)]
        s_w_split = sem("s_w_split")
        s_w_hi = sem("s_w_hi")
        s_w_used = sem("s_w_used")
        s_tr = sem("s_tr")
        s_tr_act = sem("s_tr_act")
        s_tr_dve = sem("s_tr_dve")
        s_ln = sem("s_ln")
        s_ln_sqrt = sem("s_ln_sqrt")
        s_ln_done = sem("s_ln_done")
        s_tmp = sem("s_tmp")
        s_edge = sem("s_edge")
        s_edge_tr = sem("s_edge_tr")
        s_hot = sem("s_hot")
        s_hot_free = sem("s_hot_free")
        s_win = sem("s_win")
        s_win_free = sem("s_win_free")
        s_agg = sem("s_agg")
        s_agg_dve = sem("s_agg_dve")
        s_agg_act = sem("s_agg_act")
        s_gnn = sem("s_gnn")
        s_mk = sem("s_mk")
        s_mq = sem("s_mq")
        s_mv = sem("s_mv")
        s_mmax = sem("s_mmax")
        s_mexp = sem("s_mexp")
        s_mrecip = sem("s_mrecip")
        s_mtr = sem("s_mtr")
        s_mk_out = sem("s_mk_out")
        s_mv_out = sem("s_mv_out")
        s_ctx = sem("s_ctx")
        s_ctx_out = sem("s_ctx_out")
        s_mo = sem("s_mo")
        s_mo_act = sem("s_mo_act")
        s_mo_dve = sem("s_mo_dve")
        s_mixout = sem("s_mixout")
        s_x1 = sem("s_x1")
        s_st = sem("s_st")
        s_st_xn = sem("s_st_xn")
        s_x_again = sem("s_x_again")
        s_xn_back = sem("s_xn_back")
        s_x1_back = sem("s_x1_back")
        s_xt_st = sem("s_xt_st")
        s_xt_ld = sem("s_xt_ld")
        s_pool_mm = sem("s_pool_mm")
        s_route = sem("s_route")
        s_route_act = sem("s_route_act")
        s_ld_ev = sem("s_ld_ev")
        s_k_hi = sem("s_k_hi")
        s_k_lo = sem("s_k_lo")
        s_k_copy = sem("s_k_copy")
        s_q_hi = sem("s_q_hi")
        s_q_lo = sem("s_q_lo")
        s_v = sem("s_v")
        s_vtr = sem("s_vtr")
        s_v_hi = sem("s_v_hi")
        s_v_lo = sem("s_v_lo")
        s_score = sem("s_score")
        s_taken = sem("s_taken")
        s_rowmax = sem("s_rowmax")
        s_exp = sem("s_exp")
        s_recip = sem("s_recip")
        s_prob = sem("s_prob")
        s_pt = sem("s_pt")
        s_pt_hi = sem("s_pt_hi")
        s_pt_lo = sem("s_pt_lo")
        s_pv = sem("s_pv")
        s_o_half = sem("s_o_half")
        s_o = sem("s_o")
        s_xc_hi = sem("s_xc_hi")
        s_xc_lo = sem("s_xc_lo")
        s_pj_a = sem("s_pj_a")
        s_pj_d = sem("s_pj_d")
        s_zero = sem("s_zero")
        s_b2 = sem("s_b2")
        s_gelu = sem("s_gelu")
        s_hid_hi = sem("s_hid_hi")
        s_hid = sem("s_hid")
        s_acc = sem("s_acc")
        s_sum2 = sem("s_sum2")
        s_final = sem("s_final")
        s_out = sem("s_out")

        f32 = lambda ap: ap.bitcast(F32)

        TR1 = 12
        TR2 = TR1 + NT
        TR3 = TR2 + 12
        TR4 = TR3 + NT
        TR5 = TR4 + 12
        TR6 = TR5 + NT
        GAP = {0: 0, TR2: NT, TR4: 2 * NT}
        TRD = {0: 0, TR2: 12, TR4: 24}
        TB = [(0, 4), (4, 4), (8, 2)]

        ATT = [
            ("sp", W_SP, False), ("tp", W_TP, True), ("cr", W_CR, False)]
        NBATCH = [2 * sum(g + 1 if c else 5 for g in range(5)) for _, _, c in ATT]
        DELAY = [1, 0, 1]
        DELAY_DVE = [0, 0, 0]  
        RECIP_AFTER = 1
        PLAN = [score_plan(c) for _, _, c in ATT]

        def before(a, n, of):
            return sum(of(PLAN[a][x][1]) for x in range(n))

        def so_far(a, i, n, of):
            return 4 * sum(before(x, 2 * NT, of) for x in range(a)) + before(a, 2 * NT, of) * i + before(a, n, of)

        runs_in = lambda pieces: len(runs_of(pieces))
        shifts_in = lambda pieces: int(len(runs_of(pieces)) > 1)
        BASE_B = [sum(4 * n for n in NBATCH[:a]) for a in range(3)]

        def batches(a):
            return [(g, b) for g in range(NT) for b in range(g % 5 + 1 if ATT[a][2] else 5)]

        def order(a):
            seq, steps = batches(a), []
            last = {g: m for m, (g, _) in enumerate(seq)}
            scored = [4]
            def scored_to(n):
                while scored[0] < min(n, 2 * NT):
                    steps.append(("s", scored[0], None, None))
                    scored[0] += 1
            def transposed(m):
                if m < len(seq):
                    scored_to(2 * seq[m][0] + 2)
                    steps.append(("t", m, *seq[m]))
            for m in range(AHEAD):
                transposed(m)
            for m, (g, b) in enumerate(seq):
                per_group = sum(x == g for x, _ in seq)
                if b == per_group // 2:
                    scored_to(2 * g + 5)
                steps.append(("p", m, g, b))
                if m == last[g]:
                    steps.append(("o", g, g, b))
                    scored_to(2 * g + 6)
                transposed(m + AHEAD)
            return steps

        def order_behind(a, delay):
            steps, held = [], []
            for step in order(a):
                what, _, g, _ = step
                while held and (what == "s" or what == "t" and held[0][1][1] <= 2 * g + 1):
                    steps.append(held.pop(0)[1])
                if what == "s" and delay:
                    held.append([delay, step])
                else:
                    steps.append(step)
                if what == "t":
                    for h in held:
                        h[0] -= 1
                    while held and held[0][0] <= 0:
                        steps.append(held.pop(0)[1])
            return steps + [h[1] for h in held]

        block = ctx.enter_context(nc.Block())

        @block.sync
        def _(sp):
            sp.dma_start(src_i[:, :], A["src"].rearrange("(p e) -> p e", p=NCH)).then_inc(s_ld_edge, 16)
            sp.dma_start(dst_i[:, :], A["dst"].rearrange("(p e) -> p e", p=NCH)).then_inc(s_ld_edge, 16)
            x_dram = A["x"].rearrange("(t p) d -> p t d", p=TOK)
            sp.dma_start(tok_a[:, :, :], x_dram).then_inc(s_ld_x, 16)
            sp.dma_start(vecs[:, :], A["vecs"]).then_inc(s_ld_vec, 16)

            def weights(k, slot, ago, source):
                if ago is not None:
                    sp.wait_ge(s_w_split, k - ago + 1)
                sp.dma_start(w_raw[:, slot, :], source).then_inc(s_w_raw[slot], 16)

            def block_of(name, index):
                return A[name][bass.ds(index, 1), :, :].rearrange("o p n -> (o p) n")

            for j in range(8):
                weights(W_GNN + j, SLOTS[j], since(j), block_of("w_gnn", j))
            with sp.Fori(0, 4) as i:
                for r in range(3):
                    weights(W_MIX + 3 * i + r, r, since_in_loop(W_MIX, 3, 4, r), block_of("w_mix", 4 * r + i))
            for j in range(4):
                k = W_MIXO + j
                weights(k, SLOTS[k], since(k), block_of("w_mix", 12 + j))
            sp.wait_ge(s_w_used, W_MIXO)
            sp.dma_start(x_again[:, :, :], x_dram).then_inc(s_x_again, 16)
            sp.wait_ge(s_x1, NT)
            sp.dma_start(router_w1[:, :, :], A["router_w1"]).then_inc(s_ld_router, 16)
            sp.dma_start(router_w2[:, :], A["router_w2"]).then_inc(s_ld_router, 16)
            sp.dma_start(router_b2[:, :], A["router_b2"]).then_inc(s_ld_router, 16)
            sp.dma_start(d_x1, tok_a[:, :, :]).then_inc(s_st, 16)
            sp.wait_ge(s_ln_done, 2 * NT)
            sp.dma_start(d_xn, tok_b[:, :, :]).then_inc(s_st_xn, 16)

            sp.wait_ge(s_route, ROUTE_STEPS)
            e_sp = sp.value_load(route_i[0:1, 0:1], min_val=0, max_val=EXPERTS - 1)
            e_tp = sp.value_load(route_i[0:1, 1:2], min_val=0, max_val=EXPERTS - 1)
            expert_vec = lambda name, e: A[name][bass.ds(e, 1), :, :].rearrange("o p n -> (o p) n")
            sp.dma_start(sp_vecs[:, :], expert_vec("v_sp", e_sp)).then_inc(s_ld_ev, 16)
            sp.dma_start(tp_vecs[:, :], expert_vec("v_tp", e_tp)).then_inc(s_ld_ev, 16)
            for a, (name, base, _) in enumerate(ATT):
                first = {"sp": e_sp * 16, "tp": e_tp * 16, "cr": 0}[name]
                def pass_weights(i):
                    for r in range(3):
                        weights(base + 3 * i + r, r, since_in_loop(base, 3, 4, r),
                                block_of("w_" + name, first + 4 * r + i))

                def copy_k(i):
                    for ready, part in ((s_k_hi, k_hi), (s_k_lo, k_lo)):
                        for h in range(2):
                            s, o = slice(64 * h, 64 * h + 64), slice(64 * (1 - h), 64 * (1 - h) + 64)
                            sp.wait_ge(ready, 2 * (4 * a + i) + (h + 1))
                            sp.dma_start(f32(part[o, h, :]), f32(part[s, h, :])).then_inc(s_k_copy, 16)

                pass_weights(0)
                if a == 0:
                    sp.wait_ge(s_tr_act, 24)
                    sp.wait_ge(s_tmp, 24)
                    sp.dma_start(d_xt[0], f32(xb_hi[:, :, :])).then_inc(s_xt_st, 16)
                    sp.dma_start(d_xt[1], f32(xb_lo[:, :, :])).then_inc(s_xt_st, 16)
                with sp.Fori(0, 3) as i:
                    pass_weights(i + 1)
                    copy_k(i)
                copy_k(3)
                for j in range(4):
                    k = base + 12 + j
                    weights(k, SLOTS[k], since(k), block_of("w_" + name, first + 12 + j))
                if a == 0:
                    sp.wait_ge(s_w_used, base + 12)
                    sp.wait_ge(s_xt_st, 32)
                    sp.dma_start(f32(xa_hi[:, :, :]), d_xt[0]).then_inc(s_xt_ld, 16)
                    sp.dma_start(f32(xa_lo[:, :, :]), d_xt[1]).then_inc(s_xt_ld, 16)
            sp.wait_ge(s_w_used, W_MLP)
            sp.wait_ge(s_st_xn, 16)
            sp.dma_start(tok_b[:, :, :], d_xn).then_inc(s_xn_back, 16)
            with sp.Fori(0, MLPQ) as i:
                for r in range(8):
                    weights(W_MLP + 8 * i + r, r % 3, since_in_loop(W_MLP, 8, 4, r), block_of("w_mlp", 8 * i + r))
            sp.wait_ge(s_tr, TR5)
            sp.wait_ge(s_st, 16)
            sp.dma_start(tok_b[:, :, :], d_x1).then_inc(s_x1_back, 16)
            out_dram = out.rearrange("(t p) d -> p t d", p=TOK)
            for t in range(0, NT, 2):
                sp.wait_ge(s_final, t + 2)
                sp.dma_start(out_dram[:, t:t + 2, :], tok_b[:, t:t + 2, :]).then_inc(s_out, 16)
            sp.wait_ge(s_out, 16 * NT // 2)

        @block.gpsimd
        def _(pool):
            pool.memset(ident[:, :], 0.0).then_inc(s_const, 1)
            pool.wait_ge(s_const, 1)
            pool.affine_select(out=ident[:, :], in_=ident[:, :], compare_op=ALU.not_equal, fill=1.0, base=0,
                               pattern=[[-1, 128]], channel_multiplier=1).then_inc(s_const, 1)
            pool.memset(causal_mask[:, :], 0.0).then_inc(s_const, 1)
            pool.wait_ge(s_const, 3)
            pool.affine_select(out=causal_mask[:, :], in_=causal_mask[:, :], compare_op=ALU.is_ge, fill=NEG, base=TOK,
                               pattern=[[-1, 3 * TOK]], channel_multiplier=1).then_inc(s_const, 1)
            pool.iota(iota_i[:, :], [[1, DH]], base=0, channel_multiplier=0).then_inc(s_const, 1)
            pool.iota(win_i[:, :], [[1, NW]], base=0, channel_multiplier=0).then_inc(s_const, 1)
            pool.iota(chunk_i[:, :], [[0, 1]], base=1, channel_multiplier=1).then_inc(s_const, 1)
            pool.memset(ones[:, :], 1.0).then_inc(s_const, 1)

            def carry_wait(column=20):
                return pool.tensor_tensor(pool_tick[:, column:column + 1], pool_tick[:, 21:22], pool_tick[:, 22:23], ALU.add)

            pool.memset(pool_tick[:, :], 0.0).then_inc(s_const, 1)
            pool.wait_ge(s_const, 9)

            def split(k, slot, ago, count):
                pool.wait_ge(s_w_raw[slot], 16 * count)
                if ago is not None:
                    pool.wait_ge(s_w_used, k - ago + 1)
                carry_wait()
                pool.tensor_copy(w_hi[:, slot, :], w_raw[:, slot, :]).then_inc(s_w_hi, 1)
                pool.wait_ge(s_w_hi, k + 1)
                pool.tensor_tensor(w_lo[:, slot, :], w_raw[:, slot, :], f32(w_hi[:, slot, :]), ALU.subtract)\
                    .then_inc(s_w_split, 1)

            def nth(k):
                return SLOTS[:k + 1].count(SLOTS[k])

            def split_at(k):
                split(k, SLOTS[k], since(k), nth(k))

            def split_loop(base, length, i, r):
                per_pass = sum(x % 3 == r % 3 for x in range(length))
                split(base + length * i + r, r % 3, since_in_loop(base, length, 4, r), nth(base + r) + per_pass * i)

            for j in range(8):
                split_at(W_GNN + j)
            with pool.Fori(0, 4) as i:
                for r in range(3):
                    split_loop(W_MIX, 3, i, r)
            for j in range(4):
                split_at(W_MIXO + j)
            pool.wait_ge(s_x1, NT)
            pool.memset(mean_col[:, :], 1.0 / NODES).then_inc(s_const, 1)
            pool.iota(expert_no_i[:, :], [[0, 2], [1, EXPERTS]], base=-100, channel_multiplier=0).then_inc(s_const, 1)
            for a, (_, base, causal) in enumerate(ATT):
                plan = score_plan(causal)
                for r in range(3):
                    split_at(base + r)

                def prob(n, i):
                    pool.wait_ge(s_recip, 20 * (4 * a + i) + n + 1)
                    carry_wait(n)
                    p = probs[:, n % PROBS, 0:plan[n][0]]
                    pool.tensor_scalar(p, p, stats[:, n % PROBS, 7:8], 1.0, ALU.mult, ALU.mult).then_inc(s_prob, 1)

                with pool.Fori(0, 3) as i:
                    for n in range(10):
                        prob(n, i)
                    for r in range(3):
                        split_loop(base, 3, i + 1, r)
                    for n in range(10, 20):
                        prob(n, i)
                for n in range(10):
                    prob(n, 3)
                for j in range(3):
                    split_at(base + 12 + j)
                for n in range(10, 20):
                    prob(n, 3)
                split_at(base + 15)
            with pool.Fori(0, MLPQ) as i:
                for r in range(8):
                    split_loop(W_MLP, 8, i, r)

        @block.scalar
        def _(act):
            wide = lambda b: ps[:, b:b + 3, 0:NP]
            flat = lambda ap: ap.rearrange("p (a n) -> p a n", a=3)
            act.wait_ge(s_constv, 2)

            def ln_root(n):
                act.wait_ge(s_ln, 8 * n + 3)
                act.activation(ln_r[:, 1, :], ln_r[:, 0, :], ACT.Sqrt).then_inc(s_ln_sqrt, 1)

            def banks_to_feature(base, targets):
                m = base
                for t0, nt in TB:
                    for f in range(FB):
                        act.wait_ge(s_tr, m + 1)
                        for x, (dst, sc, bi) in enumerate(targets):
                            o = dst[:, f, t0 * TOK:(t0 + nt) * TOK]
                            src = ps[:, 6 + m % 2, 0:nt * TOK]
                            if sc is None:
                                ins = act.activation(o, src, ACT.Copy)
                            else:
                                ins = act.activation(o, src, ACT.Identity, scale=vecs[:, sc + f:sc + f + 1],
                                                     bias=vecs[:, bi + f:bi + f + 1])
                        ins.then_inc(s_tr_act, 1)
                        m += 1

            ln_root(0)
            banks_to_feature(0, [(xa_hi, None, None)])

            act.activation(small[:, 6:7], small[:, 5:6], ACT.Copy).then_inc(s_win_free, 2)
            with act.Fori(0, NW // 2) as w2:
                for par in range(2):
                    act.wait_ge(s_win, 2 * w2 + (par + 1))
                    act.activation(adj[:, :, bass.ds((2 * w2 + par) * WIN, WIN)],
                                   ps[0:TOK, par, 0:DH].rearrange("p (t d) -> p t d", d=WIN), ACT.Copy)\
                        .then_inc(s_win_free, 1)
            for f in range(FB):
                act.wait_ge(s_agg_dve, 4 + 2 * f)
                act.activation(xb_hi[:, f, :], agg_tmp[:, :], ACT.Copy).then_inc(s_agg_act, 1)
            act.wait_ge(s_ld_vec, 16)
            for j in range(FB):
                act.wait_ge(s_w_used, W_GNN + 2 * j + 2)
                if j == 0:
                    act.wait_ge(s_agg_dve, 11)
                act.activation(flat(feat[:, j, :]), wide(3 * (j % 2)), ACT.Relu, bias=vecs[:, V_GNN + j:V_GNN + j + 1])\
                    .then_inc(s_gnn, 1)

            with act.Fori(0, 4) as i:
                def mix_in(dst, bank, r, s):
                    act.wait_ge(s_w_used, W_MIX + 3 * i + (r + 1))
                    act.activation(flat(dst[:, :]), wide(bank), ACT.Identity,
                                   bias=vecs[:, bass.ds(V_MIX + 4 * r + i, 1)]).then_inc(s, 1)
                mix_in(mix_k, 0, 0, s_mk)
                mix_in(mix_q, 3, 1, s_mq)
                act.wait_ge(s_mmax, i + 1)
                act.activation(mix_k[:, 0:NODES], mix_k[:, 0:NODES], ACT.Exp, bias=small[:, 0:1],
                               accum_out=small[:, 1:2]).then_inc(s_mexp, 1)
                mix_in(mix_v, 0, 2, s_mv)
                for b, (t0, nt) in enumerate(TB):
                    act.wait_ge(s_mtr, 6 * i + (b + 1))
                    act.activation(mix_kt[:, t0:t0 + nt, :], ps[0:TOK, 6 + b % 2, 0:nt * 128]
                                   .rearrange("p (t d) -> p t d", d=128), ACT.Copy).then_inc(s_mk_out, 1)
                act.wait_ge(s_mo, i + 1)
                act.activation(flat(xb_hi[:, bass.ds(i, 1), :].rearrange("p o n -> p (o n)")), wide(0), ACT.Copy)\
                    .then_inc(s_mo_act, 1)

            ln_root(1)
            ln_root(2)
            act.wait_ge(s_pool_mm, 2)
            act.activation(small[:, 4:5], ps[:, 5, 8:9], ACT.Gelu, bias=vecs[:, V_R1:V_R1 + 1]).then_inc(s_route_act, 1)
            act.wait_ge(s_route, 3)
            act.activation(route[:, 16:24], route[:, 0:8], ACT.Exp, bias=route[:, 8:9], accum_out=route[:, 9:10])\
                .then_inc(s_route_act, 1)
            banks_to_feature(TR2, [(xa_hi, V_SW, V_SB), (xb_hi, V_TW, V_TB)])

            for a, (name, base, causal) in enumerate(ATT):
                plan = score_plan(causal)
                bias, b0 = {"sp": (sp_vecs, 0), "tp": (tp_vecs, 0), "cr": (vecs, V_CIN)}[name]
                if a == 0:
                    act.wait_ge(s_ld_ev, 32)
                nb, seq = NBATCH[a], batches(a)
                with act.Fori(0, 4) as i:
                    P = 4 * a + i
                    act.wait_ge(s_w_used, base + 3 * i + 1)
                    for h in range(2):
                        lo = 64 * h
                        act.activation(flat(k_hi[lo:lo + 64, h, :]), ps[lo:lo + 64, 0:3, 0:NP], ACT.Identity,
                                       bias=bias[lo:lo + 64, bass.ds(b0 + i, 1)]).then_inc(s_k_hi, 1)
                    act.wait_ge(s_w_used, base + 3 * i + 2)
                    for h in range(2):
                        lo = 64 * h
                        act.activation(flat(q_stack[lo:lo + 64, h, :]), ps[lo:lo + 64, 3:6, 0:NP], ACT.Identity,
                                       bias=bias[lo:lo + 64, bass.ds(b0 + 4 + i, 1)]).then_inc(s_q_hi, 1)

                    def exps(n):
                        if shifts_in(plan[n][1]):
                            act.wait_ge(s_rowmax, so_far(a, i, n + 1, shifts_in))
                        act.wait_ge(s_taken, so_far(a, i, n + 1, runs_in))
                        p, st = probs[:, n % PROBS, 0:plan[n][0]], stats[:, n % PROBS, :]
                        least = 2 if shifts_in(plan[n][1]) else 0
                        act.activation(p, p, ACT.Exp, scale=-1.0, bias=st[:, least:least + 1],
                                       accum_out=st[:, 4:5]).then_inc(s_exp, 1)

                    def half_out(g):
                        h = g // 5
                        last = max(m for m, (gg, b) in enumerate(seq) if gg == g)
                        act.wait_ge(s_pv, BASE_B[a] + nb * i + (last + 1))
                        if g >= 1:
                            act.wait_ge(s_o, 10 * P + g)
                        act.activation(o_half[64 * h:64 * h + 64, :], ps[64 * (1 - h):64 * (1 - h) + 64, OUT_BANK, 0:2 * TOK],
                                       ACT.Copy).then_inc(s_o_half, 1)

                    act.wait_ge(s_w_used, base + 3 * i + 3)
                    v_bias = bias[:, bass.ds(b0 + 8 + i, 1)]
                    act.activation(v_feat[:, 2 * NP:TP], ps[:, 0, 0:NP], ACT.Identity, bias=v_bias)
                    act.activation(v_feat[:, 0:2 * NP].rearrange("p (a n) -> p a n", a=2), ps[:, 6:8, 0:NP],
                                   ACT.Identity, bias=v_bias).then_inc(s_v, 1)
                    exps(0)
                    exps(1)
                    for b, (t0, nt) in enumerate(TB):
                        act.wait_ge(s_vtr, 3 * P + (b + 1))
                        src = ps[0:TOK, 6 + b % 2, 0:nt * 128].rearrange("p (t d) -> p t d", d=128)
                        for h in range(2):
                            ins = act.activation(v_tok[:, t0:t0 + nt, h, 64 * h:64 * h + 64],
                                                 src[:, :, 64 * h:64 * h + 64], ACT.Copy)
                        ins.then_inc(s_v_hi, 1)
                    exps(2)
                    exps(3)
                    for what, m, g, b in order_behind(a, DELAY[a]):
                        if what == "s":
                            exps(m)
                        if what == "t":
                            act.wait_ge(s_pt, BASE_B[a] + nb * i + (m + 1))
                            if m >= PT:
                                act.wait_ge(s_pv, BASE_B[a] + nb * i + (m - PT + 1))
                            act.activation(pt_hi[:, m % PT, :], ps[0:TOK, T_BANK + m % T_BANKS, 0:4 * TOK], ACT.Copy)\
                                .then_inc(s_pt_hi, 1)
                        if what == "o":
                            half_out(g)
                for j in range(FB):
                    act.wait_ge(s_o, 40 * (a + 1))
                    act.activation(xc_hi[:, j, :], feat[:, j, :], ACT.Copy).then_inc(s_xc_hi, 1)
                for j in range(FB):
                    if name == "sp":
                        act.wait_ge(s_xt_st, 32)
                        act.wait_ge(s_w_used, base + 12 + j + 1)
                        act.activation(flat(xb_hi[:, j, :]), wide(3 * (j % 2)), ACT.Identity,
                                       bias=sp_vecs[:, 12 + j:13 + j]).then_inc(s_pj_a, 1)
                    elif name == "tp":
                        act.wait_ge(s_pj_d, 4 + 3 * j + 2)
                        act.activation(xa_hi[:, j, :], proj_tmp[:, :], ACT.Copy).then_inc(s_pj_a, 1)
                    else:
                        act.wait_ge(s_w_used, base + 12 + j + 1)
                        act.wait_ge(s_xc_lo, 4 * (a + 1))
                        act.activation(flat(feat[:, j, :]), wide(3 * (j % 2)), ACT.Identity,
                                       bias=vecs[:, V_COUT + j:V_COUT + j + 1]).then_inc(s_pj_a, 1)

            ln_root(3)
            banks_to_feature(TR4, [(xa_hi, V_MW, V_MB)])
            act.wait_ge(s_zero, 1)
            for j in range(FB):
                act.activation(feat[:, j, :], feat[:, j, :], ACT.Identity, bias=vecs[:, V_M2 + j:V_M2 + j + 1])\
                    .then_inc(s_b2, 1)
            with act.Fori(0, MLPQ) as i:
                for r in range(4):
                    act.wait_ge(s_w_used, W_MLP + 8 * i + (r + 1))
                    if r >= 2:
                        act.wait_ge(s_hid, 4 * i + (r - 1))
                    act.activation(flat(mlp_tmp[:, r % 2, :]), wide(3 * (r % 2)), ACT.Gelu,
                                   bias=vecs[:, bass.ds(V_M1 + 4 * i + r, 1)]).then_inc(s_gelu, 1)
                act.wait_ge(s_hid, 4 * i + 4)

        @block.vector
        def _(dve):
            wide = lambda b: ps[:, b:b + 3, 0:NP]
            flat = lambda ap: ap.rearrange("p (a n) -> p a n", a=3)
            dve.memset(f32(xa_hi[:, :, NODES:TP]), 0.0)
            dve.memset(f32(xa_lo[:, :, NODES:TP]), 0.0)
            dve.memset(small[:, :], 0.0).then_inc(s_constv, 1)
            dve.wait_ge(s_const, 2)
            dve.tensor_copy(identb[:, :], ident[:, :]).then_inc(s_constv, 1)

            def norm(n, src, dst):
                for t in range(NT):
                    ins = dve.bn_stats(ln_stats[:, t, :], src[:, t, :])
                ins.then_inc(s_ln, 1)
                dve.wait_ge(s_ln, 8 * n + 1)
                for t in range(NT):
                    ins = dve.bn_aggr(ln_mv[:, t, :], ln_stats[:, t, :])
                ins.then_inc(s_ln, 1)
                dve.wait_ge(s_ln, 8 * n + 2)
                v, r, q, h = (ln_r[:, x, :] for x in range(4))
                dve.tensor_scalar(v, ln_mv[:, :, 1], EPS, None, ALU.add).then_inc(s_ln, 1)
                dve.wait_ge(s_ln_sqrt, n + 1)
                dve.reciprocal(q, r).then_inc(s_ln, 1)
                dve.wait_ge(s_ln, 8 * n + 4)
                dve.tensor_tensor(h, q, q, ALU.mult).then_inc(s_ln, 1)
                dve.wait_ge(s_ln, 8 * n + 5)
                dve.tensor_tensor(h, h, v, ALU.mult).then_inc(s_ln, 1)
                dve.wait_ge(s_ln, 8 * n + 6)
                dve.tensor_scalar(h, h, -0.5, 1.5, ALU.mult, ALU.add).then_inc(s_ln, 1)
                dve.wait_ge(s_ln, 8 * n + 7)
                dve.tensor_tensor(r, q, h, ALU.mult).then_inc(s_ln, 1)
                dve.wait_ge(s_ln, 8 * n + 8)
                for t in range(NT):
                    dve.tensor_scalar(dst[:, t, :], src[:, t, :], ln_mv[:, t, 0:1], ln_r[:, 1, t:t + 1],
                                      ALU.subtract, ALU.mult).then_inc(s_ln_done, 1)

            def banks_to_feature(base, targets):
                m = base
                for t0, nt in TB:
                    for f in range(FB):
                        dve.wait_ge(s_tr_act, m - GAP[base] + 1)
                        span = slice(t0 * TOK, (t0 + nt) * TOK)
                        src = ps[:, 6 + m % 2, 0:nt * TOK]
                        if targets[0][2] is None:
                            hi, lo = targets[0][:2]
                            dve.tensor_tensor(lo[:, f, span], src, f32(hi[:, f, span]), ALU.subtract).then_inc(s_tr_dve, 1)
                        else:
                            written = {TR2: 0, TR4: 24}[base] + len(targets) * (m - base)
                            if written:
                                dve.wait_ge(s_tmp, written)
                            for x, (hi, lo, sc, bi) in enumerate(targets):
                                ins = dve.tensor_scalar(norm_tmp[:, x, 0:nt * TOK], src, vecs[:, sc + f:sc + f + 1],
                                                        vecs[:, bi + f:bi + f + 1], ALU.mult, ALU.add)
                            ins.then_inc(s_tr_dve, 1)
                            dve.wait_ge(s_tr_dve, m - GAP[base] + 1)
                            for x, (hi, lo, sc, bi) in enumerate(targets):
                                ins = dve.tensor_tensor(lo[:, f, span], norm_tmp[:, x, 0:nt * TOK], f32(hi[:, f, span]),
                                                        ALU.subtract)
                                ins.then_inc(s_tmp, 1)
                        m += 1

            dve.wait_ge(s_ld_x, 16)
            norm(0, tok_a, tok_a)
            banks_to_feature(0, [(xa_hi, xa_lo, None, None)])

            done = [0]

            def step(ins):
                done[0] += 1
                ins.then_inc(s_edge, 1)
                dve.wait_ge(s_edge, done[0])

            dve.wait_ge(s_ld_edge, 32)
            dve.wait_ge(s_const, 8)
            step(dve.tensor_copy(src_f[:, :], src_i[:, :]))
            step(dve.tensor_copy(dst_f[:, :], dst_i[:, :]))
            step(dve.tensor_scalar(src_tile[:, :], src_f[:, :], -(TOK - 1) / 2, 1.0 / TOK, ALU.add, ALU.mult))
            step(dve.tensor_scalar(src_tile[:, :], src_tile[:, :], MAGIC, -MAGIC, ALU.add, ALU.add))
            step(dve.tensor_scalar(dst_win[:, :], dst_f[:, :], -(WIN - 1) / 2, 1.0 / WIN, ALU.add, ALU.mult))
            step(dve.tensor_scalar(dst_win[:, :], dst_win[:, :], MAGIC, -MAGIC, ALU.add, ALU.add))
            step(dve.scalar_tensor_tensor(src_low[:, :], src_tile[:, :], -float(TOK), src_f[:, :], ALU.mult, ALU.add))
            step(dve.scalar_tensor_tensor(edge_key[:, :], src_tile[:, :], float(WIN), dst_f[:, :], ALU.mult, ALU.add))
            step(dve.scalar_tensor_tensor(edge_key[:, :], dst_win[:, :], float(WSHIFT - WIN), edge_key[:, :],
                                          ALU.mult, ALU.add))
            assert done[0] == EDGE_KEYS
            step(dve.tensor_reduce(chunk_f[0:NCH, 1:2], dst_win[:, :], AX.X, ALU.min))
            step(dve.tensor_reduce(chunk_f[0:NCH, 2:3], dst_win[:, :], AX.X, ALU.max))
            step(dve.tensor_copy(chunk_f[:, 0:1], chunk_i[:, :]))
            step(dve.tensor_scalar(chunk_f[:, 3:4], chunk_f[:, 0:1], -1001.0, None, ALU.add))
            step(dve.tensor_copy(iota_h[:, :], iota_i[:, :]))
            step(dve.tensor_copy(win_no[:, :], win_i[:, :]))
            step(dve.tensor_scalar(win_key[:, :], win_no[:, :], float(WSHIFT), None, ALU.mult))
            step(dve.tensor_scalar(inside[:, 0, :], win_no[0:NCH, :], chunk_f[0:NCH, 1:2], None, ALU.is_ge))
            step(dve.tensor_scalar(inside[:, 1, :], win_no[0:NCH, :], chunk_f[0:NCH, 2:3], None, ALU.is_le))
            step(dve.tensor_tensor(inside[:, 2, :], inside[:, 0, :], inside[:, 1, :], ALU.mult))
            step(dve.tensor_scalar(inside[:, 0, :], inside[:, 2, :], chunk_f[0:NCH, 3:4], 1000.0, ALU.mult, ALU.add))
            step(dve.tensor_scalar(inside[:, 1, :], inside[:, 2, :], chunk_f[0:NCH, 0:1], None, ALU.mult))
            assert done[0] == EDGE_INSIDE
            dve.wait_ge(s_edge_tr, 2)
            step(dve.tensor_copy(low_t[:, :, :], ps[0:ET, 0, 0:NCH * CH].rearrange("e (c p) -> e p c", c=CH)))
            step(dve.tensor_copy(key_t[:, :, :], ps[0:ET, 1, 0:NCH * CH].rearrange("e (c p) -> e p c", c=CH)))
            dve.wait_ge(s_edge_tr, 3)
            step(dve.tensor_reduce(bounds_c[:, 0:1], ps[0:NW, 2, 0:NCH], AX.X, ALU.min))
            step(dve.tensor_reduce(bounds_c[:, 1:2], ps[0:NW, 2, 128:128 + NCH], AX.X, ALU.max))
            assert done[0] == EDGE_BOUNDS
            dve.wait_ge(s_edge_tr, 4)
            step(dve.tensor_scalar(bounds_r[:, 0, :], ps[0:1, 3, 0:NW], float(NCH - 3), None, ALU.min))
            step(dve.scalar_tensor_tensor(bounds_r[:, 1, :], bounds_r[:, 0, :], 3.0, ps[0:1, 3, 64:64 + NW],
                                          ALU.add, ALU.max))
            done[0] += 1
            dve.tensor_copy(bounds_i[:, :], bounds_r[:, :, :].rearrange("o a w -> o (a w)")).then_inc(s_edge, 1)
            dve.wait_ge(s_edge, done[0])
            assert done[0] == EDGE_DONE
            dve.tensor_copy(small[:, 7:8], small[:, 5:6]).then_inc(s_hot_free, 2)

            count = dve.alloc_register("hot_count")
            dve.reg_mov(count, 0)

            def chunk_rows(w, p):
                n = dve.snap(count, min_val=0, max_val=NCH * NW)
                dve.wait_ge(s_hot_free, n + 1)
                for c in range(CH):
                    row = onehot[:, bass.ds((n % 2) * CH + c, 1), :].rearrange("p o n -> p (o n)")
                    low = low_t[:, bass.ds(p, 1), c:c + 1].rearrange("p o c -> p (o c)")
                    key = key_t[:, bass.ds(p, 1), c:c + 1].rearrange("p o c -> p (o c)")
                    dve.tensor_scalar(row[:, 0:ET], iota_h[0:ET, 0:ET], low, None, ALU.is_equal)
                    ins = dve.tensor_scalar(row[:, ET:ET + DH], iota_h[0:ET, :], win_key[0:ET, bass.ds(w, 1)], key,
                                            ALU.add, ALU.is_equal)
                ins.then_inc(s_hot, 1)
                dve.reg_add(count, count, 1)

            with dve.Fori(0, NW) as w:
                lo = dve.value_load(bounds_i[0:1, bass.ds(w, 1)], min_val=0, max_val=NCH - 3)
                hi = dve.value_load(bounds_i[0:1, bass.ds(w + NW, 1)], min_val=3, max_val=NCH)
                with dve.Fori(lo, hi) as p:
                    chunk_rows(w, p)

            dve.wait_ge(s_win_free, NW + 2)
            dve.tensor_reduce(deg_part[:, :], adj[:, :, :].rearrange("p t d -> p d t"), AX.X, ALU.add)\
                .then_inc(s_agg_dve, 1)
            dve.wait_ge(s_agg, 2)
            dve.tensor_scalar(flat(agg_tmp[:, :]), wide(3), 1.0, None, ALU.max).then_inc(s_agg_dve, 1)
            dve.wait_ge(s_agg_dve, 2)
            dve.reciprocal(inv_deg[:, :], agg_tmp[:, :]).then_inc(s_agg_dve, 1)
            for f in range(FB):
                dve.wait_ge(s_agg, AGG_OF[f] + 1)
                dve.wait_ge(s_agg_dve, 3 + 2 * f)
                if f:
                    dve.wait_ge(s_agg_act, f)
                dve.tensor_tensor(flat(agg_tmp[:, :]), wide(AGG_BANK[f]), flat(inv_deg[:, :]), ALU.mult)\
                    .then_inc(s_agg_dve, 1)
                dve.wait_ge(s_agg_act, f + 1)
                dve.tensor_tensor(xb_lo[:, f, :], agg_tmp[:, :], f32(xb_hi[:, f, :]), ALU.subtract).then_inc(s_agg_dve, 1)

            dve.memset(context[:, :], 0.0)
            with dve.Fori(0, 4) as i:
                dve.wait_ge(s_mk, i + 1)
                dve.tensor_reduce(small[:, 0:1], mix_k[:, 0:NODES], AX.X, ALU.max, negate=True).then_inc(s_mmax, 1)
                dve.wait_ge(s_mexp, i + 1)
                dve.reciprocal(small[:, 2:3], small[:, 1:2]).then_inc(s_mrecip, 1)
                for b, (t0, nt) in enumerate(TB):
                    dve.wait_ge(s_mtr, 6 * i + (3 + b + 1))
                    dve.tensor_copy(mix_vt[:, t0:t0 + nt, :], ps[0:TOK, 6 + (b + 1) % 2, 0:nt * 128]
                                    .rearrange("p (t d) -> p t d", d=128)).then_inc(s_mv_out, 1)
                dve.wait_ge(s_ctx, i + 1)
                dve.wait_ge(s_mrecip, i + 1)
                for h in range(2):
                    s = slice(64 * h, 64 * h + 64)
                    ins = dve.tensor_scalar(context[s, s], ps[s, 3, s], small[s, 2:3], None, ALU.mult)
                ins.then_inc(s_ctx_out, 1)
                dve.wait_ge(s_mo_act, i + 1)
                one = lambda t: t[:, bass.ds(i, 1), :].rearrange("p o n -> p (o n)")
                dve.tensor_tensor(flat(one(xb_lo)), wide(0), flat(f32(one(xb_hi))), ALU.subtract).then_inc(s_mo_dve, 1)
            for j in range(FB):
                dve.wait_ge(s_w_used, W_MIXO + j + 1)
                dve.scalar_tensor_tensor(flat(feat[:, j, :]), wide(3 * (j % 2)), vecs[:, V_MIXO + j:V_MIXO + j + 1],
                                         flat(feat[:, j, :]), ALU.add, ALU.add).then_inc(s_mixout, 1)

            dve.wait_ge(s_x_again, 16)
            for t in range(NT):
                dve.wait_ge(s_tr, TR1 + t + 1)
                dve.tensor_tensor(tok_a[:, t, :], ps[0:TOK, 6 + t % 2, :], x_again[:, t, :], ALU.add).then_inc(s_x1, 1)
            dve.wait_ge(s_x1, NT)
            dve.memset(f32(xa_hi[:, :, NODES:TP]), 0.0)
            dve.memset(f32(xa_lo[:, :, NODES:TP]), 0.0)
            norm(1, tok_a, tok_b)
            dve.wait_ge(s_st, 16)
            dve.wait_ge(s_ln_done, 2 * NT)
            norm(2, tok_b, tok_a)

            dve.wait_ge(s_pool_mm, 1)
            dve.tensor_copy(pooled[:, :], ps[:, 5, 0:FB]).then_inc(s_route, 1)
            dve.wait_ge(s_pool_mm, 3)
            dve.wait_ge(s_ld_router, 48)
            dve.tensor_tensor(route[:, 0:8], ps[0:1, 5, 16:24], router_b2[:, :], ALU.add).then_inc(s_route, 1)
            dve.wait_ge(s_route, 2)
            dve.tensor_reduce(route[:, 8:9], route[:, 0:8], AX.X, ALU.max, negate=True).then_inc(s_route, 1)
            dve.wait_ge(s_route_act, 2)
            dve.reciprocal(route[:, 10:11], route[:, 9:10]).then_inc(s_route, 1)
            dve.wait_ge(s_route, 4)
            dve.tensor_scalar(route[:, 24:32], route[:, 16:24], route[:, 10:11], None, ALU.mult).then_inc(s_route, 1)
            dve.wait_ge(s_route, 5)
            dve.tensor_reduce(route[:, 32:34], route[:, 24:32].rearrange("o (a n) -> o a n", a=2), AX.X, ALU.max)\
                .then_inc(s_route, 1)
            dve.wait_ge(s_route, 6)
            dve.wait_ge(s_const, 11)
            for h in range(2):
                ins = dve.tensor_scalar(route[:, 40 + 4 * h:44 + 4 * h], route[:, 24 + 4 * h:28 + 4 * h],
                                        route[:, 32 + h:33 + h], None, ALU.is_ge)
            dve.tensor_copy(expert_no[:, :], expert_no_i[:, :]).then_inc(s_route, 1)
            dve.wait_ge(s_route, 7)
            dve.tensor_tensor(route[:, 48:56], route[:, 40:48], expert_no[:, :], ALU.mult).then_inc(s_route, 1)
            dve.wait_ge(s_route, 8)
            dve.tensor_reduce(route[:, 56:58], route[:, 48:56].rearrange("o (a n) -> o a n", a=2), AX.X, ALU.min)\
                .then_inc(s_route, 1)
            dve.wait_ge(s_route, 9)
            dve.tensor_scalar(route_i[:, :], route[:, 56:58], 100.0, None, ALU.add).then_inc(s_route, 1)
            banks_to_feature(TR2, [(xa_hi, xa_lo, V_SW, V_SB), (xb_hi, xb_lo, V_TW, V_TB)])

            for a, (name, base, causal) in enumerate(ATT):
                plan = score_plan(causal)
                bias, b0 = {"sp": (sp_vecs, 0), "tp": (tp_vecs, 0), "cr": (vecs, V_CIN)}[name]
                if a == 0:
                    dve.wait_ge(s_ld_ev, 32)
                nb, seq = NBATCH[a], batches(a)
                with dve.Fori(0, 4) as i:
                    P = 4 * a + i
                    for h in range(2):
                        s = slice(64 * h, 64 * h + 64)
                        dve.wait_ge(s_k_hi, 2 * P + (h + 1))
                        dve.scalar_tensor_tensor(flat(k_lo[s, h, :]), ps[s, 0:3, 0:NP], bias[s, bass.ds(b0 + i, 1)],
                                                 flat(f32(k_hi[s, h, :])), ALU.add, ALU.subtract).then_inc(s_k_lo, 1)
                    for h in range(2):
                        s, o = slice(64 * h, 64 * h + 64), slice(64 * (1 - h), 64 * (1 - h) + 64)
                        dve.wait_ge(s_q_hi, 2 * P + (h + 1))
                        dve.scalar_tensor_tensor(flat(q_stack[o, h, :]), ps[s, 3:6, 0:NP],
                                                 bias[s, bass.ds(b0 + 4 + i, 1)], flat(f32(q_stack[s, h, :])),
                                                 ALU.add, ALU.subtract).then_inc(s_q_lo, 1)

                    def shift(n):
                        st = stats[:, n % PROBS, :]
                        if n >= PROBS:
                            last = max(m for m, (g, b) in enumerate(seq) if g == (n - PROBS) // 2)
                            dve.wait_ge(s_pt, BASE_B[a] + nb * i + (last + 1))
                        banks = 0
                        for x, (b, nbk, first, w) in enumerate(runs_of(plan[n][1])):
                            banks += nbk
                            dve.wait_ge(s_score, so_far(a, i, n, len) + banks)
                            o = probs[:, n % PROBS, first:first + nbk * w].rearrange("p (b n) -> p b n", b=nbk)
                            dve.tensor_scalar(o, ps[0:TOK, b:b + nbk, 0:w], -SCALE, None, ALU.mult, ALU.min,
                                              accum_out=st[:, x:x + 1]).then_inc(s_taken, 1)
                        if shifts_in(plan[n][1]):
                            dve.wait_ge(s_taken, so_far(a, i, n + 1, runs_in))
                            dve.tensor_tensor(st[:, 2:3], st[:, 0:1], st[:, 1:2], ALU.min).then_inc(s_rowmax, 1)

                    def recip(n):
                        st = stats[:, n % PROBS, :]
                        dve.wait_ge(s_exp, 20 * P + (n + 1))
                        dve.reciprocal(st[:, 7:8], st[:, 4:5]).then_inc(s_recip, 1)

                    def out_tiles(g):
                        s = slice(64 * (g // 5), 64 * (g // 5) + 64)
                        dve.wait_ge(s_o_half, 10 * P + (g + 1))
                        o = feat[s, bass.ds(i, 1), 2 * TOK * (g % 5):2 * TOK * (g % 5 + 1)].rearrange("p o n -> p (o n)")
                        dve.tensor_tensor(o, ps[s, OUT_BANK, 0:2 * TOK], o_half[s, :], ALU.add).then_inc(s_o, 1)

                    shift(0)
                    recip(0)
                    shift(1)
                    for b, (t0, nt) in enumerate(TB):
                        dve.wait_ge(s_v_hi, 3 * P + (b + 1))
                        src = ps[0:TOK, 6 + b % 2, 0:nt * 128].rearrange("p (t d) -> p t d", d=128)
                        for h in range(2):
                            s, o = slice(64 * h, 64 * h + 64), slice(64 * (1 - h), 64 * (1 - h) + 64)
                            ins = dve.tensor_tensor(v_tok[:, t0:t0 + nt, h, o], src[:, :, s],
                                                    f32(v_tok[:, t0:t0 + nt, h, s]), ALU.subtract)
                        ins.then_inc(s_v_lo, 1)
                    recip(1)
                    shift(2)
                    recip(2)
                    shift(3)
                    late = [[3, 0]]
                    for what, m, g, b in order_behind(a, DELAY_DVE[a]):
                        if what == "s":
                            shift(m)
                            late.append([m, RECIP_AFTER])
                        if what == "t":
                            while late and (late[0][0] <= 2 * g + 1 or late[0][1] <= 0):
                                recip(late.pop(0)[0])
                            for x in late:
                                x[1] -= 1
                            dve.wait_ge(s_pt_hi, BASE_B[a] + nb * i + (m + 1))
                            if m >= PT:
                                dve.wait_ge(s_pv, BASE_B[a] + nb * i + (m - PT + 1))
                            dve.tensor_tensor(pt_lo[:, m % PT, :], ps[0:TOK, T_BANK + m % T_BANKS, 0:4 * TOK],
                                              f32(pt_hi[:, m % PT, :]), ALU.subtract).then_inc(s_pt_lo, 1)
                        if what == "o":
                            out_tiles(g)
                    while late:
                        recip(late.pop(0)[0])
                for j in range(FB):
                    dve.wait_ge(s_xc_hi, 4 * a + j + 1)
                    dve.tensor_tensor(xc_lo[:, j, :], feat[:, j, :], f32(xc_hi[:, j, :]), ALU.subtract)\
                        .then_inc(s_xc_lo, 1)
                for j in range(FB):
                    bank = wide(3 * (j % 2))
                    if name == "sp":
                        dve.wait_ge(s_pj_a, j + 1)
                        dve.scalar_tensor_tensor(flat(xb_lo[:, j, :]), bank, sp_vecs[:, 12 + j:13 + j],
                                                 flat(f32(xb_hi[:, j, :])), ALU.add, ALU.subtract).then_inc(s_pj_d, 1)
                    if name == "tp":
                        dve.wait_ge(s_w_used, base + 12 + j + 1)
                        if j:
                            dve.wait_ge(s_pj_d, 4 + 3 * j)
                        dve.scalar_tensor_tensor(flat(proj_tmp[:, :]), bank, tp_vecs[:, 12 + j:13 + j],
                                                 flat(f32(xa_hi[:, j, :])), ALU.add, ALU.add).then_inc(s_pj_d, 1)
                        dve.wait_ge(s_pj_d, 4 + 3 * j + 1)
                        dve.tensor_tensor(proj_tmp[:, :], proj_tmp[:, :], f32(xa_lo[:, j, :]), ALU.add).then_inc(s_pj_d, 1)
                        dve.wait_ge(s_pj_a, 4 + j + 1)
                        dve.tensor_tensor(xa_lo[:, j, :], proj_tmp[:, :], f32(xa_hi[:, j, :]), ALU.subtract)\
                            .then_inc(s_pj_d, 1)

            dve.wait_ge(s_xn_back, 16)
            for t in range(NT):
                dve.wait_ge(s_tr, TR3 + t + 1)
                dve.tensor_tensor(tok_a[:, t, :], ps[0:TOK, 6 + t % 2, :], tok_b[:, t, :], ALU.add).then_inc(s_x1, 1)
            dve.memset(feat[:, :, :], 0.0).then_inc(s_zero, 1)
            dve.wait_ge(s_x1, 2 * NT)
            norm(3, tok_a, tok_b)
            banks_to_feature(TR4, [(xa_hi, xa_lo, V_MW, V_MB)])
            dve.wait_ge(s_b2, FB)
            with dve.Fori(0, MLPQ) as i:
                for r in range(4):
                    dve.wait_ge(s_gelu, 4 * i + (r + 1))
                    dve.tensor_copy(xb_hi[:, r, :], mlp_tmp[:, r % 2, :]).then_inc(s_hid_hi, 1)
                    dve.wait_ge(s_hid_hi, 4 * i + (r + 1))
                    dve.tensor_tensor(xb_lo[:, r, :], mlp_tmp[:, r % 2, :], f32(xb_hi[:, r, :]), ALU.subtract)\
                        .then_inc(s_hid, 1)
                for r in range(4):
                    dve.wait_ge(s_w_used, W_MLP + 8 * i + (4 + r + 1))
                    f = flat(feat[:, r, :])
                    dve.tensor_tensor(f, wide(3 * (r % 2)), f, ALU.add).then_inc(s_acc, 1)
            dve.wait_ge(s_x1_back, 16)
            for t in range(NT):
                dve.wait_ge(s_tr, TR5 + t + 1)
                dve.tensor_tensor(tok_a[:, t, :], ps[0:TOK, 6 + t % 2, :], tok_a[:, t, :], ALU.add).then_inc(s_sum2, 1)
                dve.wait_ge(s_sum2, t + 1)
                dve.tensor_tensor(tok_b[:, t, :], tok_a[:, t, :], tok_b[:, t, :], ALU.add).then_inc(s_final, 1)

        @block.tensor
        def _(pe):
            def linear(k, slot, x_hi, x_lo, bank, first=True, last=True):
                pe.wait_ge(s_w_split, k + 1)
                parts = ((w_hi, x_hi), (w_hi, x_lo), (w_lo, x_hi))
                for c in range(FB):
                    for n, (w, x) in enumerate(parts):
                        for p in range(3):
                            ins = pe.matmul(ps[:, (bank + p) % 8, 0:NP], w[:, slot, 128 * c:128 * c + 128],
                                            x[:, c, NP * p:NP * p + NP], start=(first and c == 0 and n == 0),
                                            stop=(last and c == FB - 1 and n == 2))
                ins.then_inc(s_w_used, 1)

            def to_feature(base, norm_no, src):
                m = base
                for t0, nt in TB:
                    pe.wait_ge(s_ln_done, NT * norm_no + t0 + nt)
                    for f in range(FB):
                        if m - base >= 2:
                            pe.wait_ge(s_tr_dve, TRD[base] + (m - base) - 1)
                        for t in range(nt):
                            ins = pe.transpose(ps[:, 6 + m % 2, t * TOK:(t + 1) * TOK],
                                               src[:, t0 + t, 128 * f:128 * f + 128], ident[0:TOK, 0:TOK])
                        ins.then_inc(s_tr, 1)
                        m += 1

            def to_nodes(base, readers, read_base):
                for t in range(NT):
                    if t >= 2:
                        pe.wait_ge(readers, read_base + t - 1)
                    for f in range(FB):
                        ins = pe.transpose(ps[0:TOK, 6 + t % 2, 128 * f:128 * f + 128],
                                           feat[:, f, t * TOK:(t + 1) * TOK], ident[:, :])
                    ins.then_inc(s_tr, 1)

            pe.wait_ge(s_constv, 2)
            to_feature(0, 0, tok_a)

            pe.wait_ge(s_edge, EDGE_KEYS)
            for x, src in enumerate((src_low, edge_key)):
                for c in range(CH):
                    ins = pe.transpose(ps[0:ET, x, c * NCH:(c + 1) * NCH], src[:, c * ET:(c + 1) * ET], ident[0:NCH, 0:NCH])
                ins.then_inc(s_edge_tr, 1)
            pe.wait_ge(s_edge, EDGE_INSIDE)
            for x in range(2):
                ins = pe.transpose(ps[0:NW, 2, 128 * x:128 * x + NCH], inside[:, x, :], ident[0:NCH, 0:NCH])
            ins.then_inc(s_edge_tr, 1)
            pe.wait_ge(s_edge, EDGE_BOUNDS)
            for x in range(2):
                ins = pe.transpose(ps[0:1, 3, 64 * x:64 * x + NW], bounds_c[:, x:x + 1], ident[0:NW, 0:NW])
            ins.then_inc(s_edge_tr, 1)
            pe.wait_ge(s_edge, EDGE_DONE)

            count = pe.alloc_register("hot_used")
            pe.reg_mov(count, 0)

            def chunk_counts(bank, first, last):
                n = pe.snap(count, min_val=0, max_val=NCH * NW)
                pe.wait_ge(s_hot, n + 1)
                for c in range(CH):
                    row = onehot[:, bass.ds((n % 2) * CH + c, 1), :].rearrange("p o n -> p (o n)")
                    ins = pe.matmul(ps[0:ET, bank, 0:DH], row[:, 0:ET], row[:, ET:ET + DH],
                                    start=(first and c == 0), stop=(last and c == CH - 1), skip_group_check=True)
                ins.then_inc(s_hot_free, 1)
                if last:
                    pe.matmul(ps[0:1, 4, 0:1], identb[:, 0:1], identb[:, 0:1], start=True, stop=True).then_inc(s_win, 1)
                pe.reg_add(count, count, 1)

            with pe.Fori(0, NW // 2) as w2:
                for par in range(2):
                    w = 2 * w2 + par
                    lo = pe.value_load(bounds_i[0:1, bass.ds(w, 1)], min_val=0, max_val=NCH - 3)
                    hi = pe.value_load(bounds_i[0:1, bass.ds(w + NW, 1)], min_val=3, max_val=NCH)
                    pe.wait_ge(s_win_free, w + 1)
                    chunk_counts(par, True, False)
                    with pe.Fori(lo + 1, hi - 1):
                        chunk_counts(par, False, False)
                    chunk_counts(par, False, True)

            pe.wait_ge(s_win_free, NW + 2)

            def aggregate(f, bank):
                for t in range(NT):
                    for p in range(3):
                        ins = pe.matmul(ps[:, bank + p, 0:NP], tok_a[:, t, 128 * f:128 * f + 128],
                                        adj[:, t, NP * p:NP * p + NP], start=(t == 0), stop=(t == NT - 1))
                ins.then_inc(s_agg, 1)

            aggregate(0, 0)
            pe.wait_ge(s_agg_dve, 1)
            for p in range(3):
                ins = pe.matmul(ps[:, 3 + p, 0:NP], ones[0:TOK, :], deg_part[:, NP * p:NP * p + NP], start=True, stop=True)
            ins.then_inc(s_agg, 1)
            pe.wait_ge(s_agg_dve, 4)
            aggregate(1, 0)
            aggregate(2, 3)
            pe.wait_ge(s_agg_dve, 6)
            aggregate(3, 0)

            for j in range(FB):
                if j >= 2:
                    pe.wait_ge(s_gnn, j - 1)
                if j == 0:
                    pe.wait_ge(s_agg_dve, 11)
                    pe.wait_ge(s_tr_dve, 12)
                linear(W_GNN + 2 * j, SLOTS[2 * j], xa_hi, xa_lo, 3 * (j % 2), last=False)
                linear(W_GNN + 2 * j + 1, SLOTS[2 * j + 1], xb_hi, xb_lo, 3 * (j % 2), first=False)

            pe.wait_ge(s_gnn, 4)
            with pe.Fori(0, 4) as i:
                linear(W_MIX + 3 * i, 0, xa_hi, xa_lo, 0)
                linear(W_MIX + 3 * i + 1, 1, xa_hi, xa_lo, 3)
                pe.wait_ge(s_mk, i + 1)
                linear(W_MIX + 3 * i + 2, 2, xa_hi, xa_lo, 0)
                for m in range(6):
                    src, (t0, nt) = (mix_k if m < 3 else mix_v), TB[m % 3]
                    if m == 0:
                        pe.wait_ge(s_mexp, i + 1)
                    if m == 3:
                        pe.wait_ge(s_mv, i + 1)
                    if 2 <= m < 5:
                        pe.wait_ge(s_mk_out, 3 * i + (m - 1))
                    if m == 5:
                        pe.wait_ge(s_mv_out, 3 * i + 1)
                    for t in range(nt):
                        ins = pe.transpose(ps[0:TOK, 6 + m % 2, 128 * t:128 * t + 128],
                                           src[:, (t0 + t) * TOK:(t0 + t + 1) * TOK], ident[:, :])
                    ins.then_inc(s_mtr, 1)
                pe.wait_ge(s_mv_out, 3 * i + 3)
                pe.wait_ge(s_mq, i + 1)
                for t in range(NT):
                    ins = pe.matmul(ps[:, 3, 0:128], mix_kt[:, t, :], mix_vt[:, t, :], start=(t == 0), stop=(t == NT - 1))
                ins.then_inc(s_ctx, 1)
                pe.wait_ge(s_ctx_out, i + 1)
                for p in range(3):
                    ins = pe.matmul(ps[:, p, 0:NP], context[:, :], mix_q[:, NP * p:NP * p + NP], start=True, stop=True)
                ins.then_inc(s_mo, 1)
                pe.wait_ge(s_mo_dve, i + 1)
            for j in range(FB):
                if j >= 2:
                    pe.wait_ge(s_mixout, j - 1)
                linear(W_MIXO + j, SLOTS[W_MIXO + j], xb_hi, xb_lo, 3 * (j % 2))
            pe.wait_ge(s_mixout, 4)
            to_nodes(TR1, s_x1, 0)

            pe.wait_ge(s_ln_done, 2 * NT)
            pe.wait_ge(s_const, 11)
            for f in range(FB):
                for t in range(NT):
                    ins = pe.matmul(ps[:, 5, f:f + 1], tok_b[:, t, 128 * f:128 * f + 128], mean_col[:, :],
                                    start=(t == 0), stop=(t == NT - 1))
            ins.then_inc(s_pool_mm, 1)
            pe.wait_ge(s_route, 1)
            pe.wait_ge(s_ld_router, 48)
            for f in range(FB):
                ins = pe.matmul(ps[:, 5, 8:9], router_w1[:, f, :], pooled[:, f:f + 1], start=(f == 0), stop=(f == FB - 1))
            ins.then_inc(s_pool_mm, 1)
            pe.wait_ge(s_route_act, 1)
            pe.matmul(ps[0:1, 5, 16:24], small[:, 4:5], router_w2[:, :], start=True, stop=True).then_inc(s_pool_mm, 1)
            to_feature(TR2, 2, tok_a)

            for a, (name, base, causal) in enumerate(ATT):
                plan = score_plan(causal)
                q_hi_src, q_lo_src = (xb_hi, xb_lo) if name == "cr" else (xa_hi, xa_lo)
                nb, seq = NBATCH[a], batches(a)
                if name == "sp":
                    pe.wait_ge(s_tmp, 24)
                if name == "tp":
                    pe.wait_ge(s_xt_ld, 32)
                    pe.wait_ge(s_pj_d, 4)
                if name == "cr":
                    pe.wait_ge(s_pj_d, 16)
                with pe.Fori(0, 4) as i:
                    P = 4 * a + i
                    linear(base + 3 * i, 0, xa_hi, xa_lo, 0)
                    linear(base + 3 * i + 1, 1, q_hi_src, q_lo_src, 3)

                    def scores(n):
                        h, t = n // NT, n % NT
                        for j, (b, first, w) in enumerate(plan[n][1]):
                            users = [(x, y) for x in range(n) for y, (b0, nbk, _, _) in enumerate(runs_of(plan[x][1]))
                                     if b0 <= b < b0 + nbk]
                            if not users and b == 0:
                                pe.wait_ge(s_v, P + 1)
                            if users:
                                x, y = users[-1]
                                pe.wait_ge(s_taken, so_far(a, i, x, runs_in) + (y + 1))
                            masked = causal and j == len(plan[n][1]) - 1
                            query = q_stack[:, h, t * TOK:(t + 1) * TOK]
                            pe.matmul(ps[0:TOK, b, 0:w], query, k_hi[:, h, first:first + w], start=True, stop=False)
                            if masked:
                                off = TOK * (1 - t % 2)
                                pe.matmul(ps[0:TOK, b, w - 2 * TOK:w], identb[0:TOK, 0:TOK],
                                          causal_mask[:, off:off + 2 * TOK], start=False, stop=False,
                                          skip_group_check=True)
                            pe.matmul(ps[0:TOK, b, 0:w], query, k_lo[:, h, first:first + w], start=False, stop=True)\
                                .then_inc(s_score, 1)

                    pe.wait_ge(s_k_lo, 2 * P + 2)
                    linear(base + 3 * i + 2, 2, xa_hi, xa_lo, 6)
                    pe.wait_ge(s_q_lo, 2 * P + 2)
                    pe.wait_ge(s_k_copy, 64 * P + 64)
                    scores(0)
                    scores(1)
                    for b, (t0, nt) in enumerate(TB):
                        pe.wait_ge(s_v, P + 1)
                        if b == 2:
                            pe.wait_ge(s_v_lo, 3 * P + 1)
                        for t in range(nt):
                            ins = pe.transpose(ps[0:TOK, 6 + b % 2, 128 * t:128 * t + 128],
                                               v_feat[:, (t0 + t) * TOK:(t0 + t + 1) * TOK], ident[:, :])
                        ins.then_inc(s_vtr, 1)
                    scores(2)
                    scores(3)
                    pe.wait_ge(s_v_lo, 3 * P + 3)
                    for what, m, g, b in order(a):
                        kts = 2 * sum(x == g for x, _ in seq)
                        if what == "s":
                            scores(m)
                        if what == "t":
                            if b == 0:
                                pe.wait_ge(s_prob, 20 * P + (2 * g + 2))
                            if m >= T_BANKS:
                                pe.wait_ge(s_pt_lo, BASE_B[a] + nb * i + (m - T_BANKS + 1))
                            for x in range(4):
                                kt, n = 2 * b + x // 2, 2 * g + x % 2
                                ins = pe.transpose(ps[0:TOK, T_BANK + m % T_BANKS, x * TOK:(x + 1) * TOK],
                                                   probs[:, n % PROBS, kt * TOK:(kt + 1) * TOK], ident[0:TOK, 0:TOK])
                            ins.then_inc(s_pt, 1)
                        if what == "p":
                            pe.wait_ge(s_pt_lo, BASE_B[a] + nb * i + (m + 1))
                            if b == 0 and g >= 1:
                                pe.wait_ge(s_o, 10 * P + g)
                            for x in range(2):
                                kt = 2 * b + x
                                for part in (pt_hi, pt_lo):
                                    ins = pe.matmul(ps[:, OUT_BANK, 0:2 * TOK], v_tok[:, kt, g // 5, :],
                                                    part[:, m % PT, 2 * TOK * x:2 * TOK * (x + 1)],
                                                    start=(kt == 0 and part is pt_hi),
                                                    stop=(kt == kts - 1 and part is pt_lo))
                            ins.then_inc(s_pv, 1)
                    pe.wait_ge(s_o, 10 * P + 10)
                pe.wait_ge(s_xc_lo, 4 * (a + 1))
                for j in range(FB):
                    if j >= 2:
                        if name == "sp":
                            pe.wait_ge(s_pj_d, j - 1)
                        elif name == "tp":
                            pe.wait_ge(s_pj_d, 4 + 3 * (j - 2) + 1)
                        else:
                            pe.wait_ge(s_pj_a, 8 + j - 1)
                    linear(base + 12 + j, SLOTS[base + 12 + j], xc_hi, xc_lo, 3 * (j % 2))

            pe.wait_ge(s_pj_a, 12)
            to_nodes(TR3, s_x1, NT)
            to_feature(TR4, 3, tok_b)
            pe.wait_ge(s_tmp, 36)
            with pe.Fori(0, MLPQ) as i:
                for r in range(4):
                    if r >= 2:
                        pe.wait_ge(s_gelu, 4 * i + (r - 1))
                    linear(W_MLP + 8 * i + r, r % 3, xa_hi, xa_lo, 3 * (r % 2))
                for r in range(4):
                    if r < 2:
                        pe.wait_ge(s_gelu, 4 * i + (r + 3))
                    else:
                        pe.wait_ge(s_acc, 4 * i + (r - 1))
                    if r == 0:
                        pe.wait_ge(s_hid, 4 * i + 4)
                    linear(W_MLP + 8 * i + 4 + r, (4 + r) % 3, xb_hi, xb_lo, 3 * (r % 2))
                pe.wait_ge(s_acc, 4 * i + 4)
            to_nodes(TR5, s_sum2, 0)


def kernel(**inputs):
    import concourse.bacc as bacc
    from concourse.bass_utils import run_bass_kernel_spmd

    g = {k: np.asarray(v) for k, v in inputs.items()}

    def blocks(w):
        o, n = w.shape[-2:]
        w = w.reshape(-1, o // 128, 128, n // 512, 4, 128)
        return w.transpose(0, 1, 3, 5, 4, 2)

    def flat(b):
        return np.ascontiguousarray(b).reshape(-1, 128, BLK)

    def columns(v):
        return np.swapaxes(v.reshape(v.shape[:-1] + (-1, 128)), -1, -2)

    def kqv(w):
        q, k, v = np.split(w, 3, axis=-2)
        return np.concatenate([k, q, v], axis=-2)

    def kqv_b(v):
        q, k, w = np.split(v, 3, axis=-1)
        return np.concatenate([k, q, w], axis=-1)

    p = "L0_ffn_"
    w1 = blocks(g[p + "mlp_w1"])[0, :, 0].reshape(MLPQ, 4, 128, 4, 128)
    w2 = blocks(g[p + "mlp_w2"])[0].transpose(1, 0, 2, 3, 4)
    experts = lambda qkv, o: np.ascontiguousarray(np.concatenate([qkv, o], axis=1)).reshape(-1, 128, BLK)
    e4 = lambda w: blocks(w).reshape(EXPERTS, -1, 128, BLK)
    arrays = {
        "x": np.ascontiguousarray(g["x"]),
        "src": np.ascontiguousarray(g["src"]),
        "dst": np.ascontiguousarray(g["dst"]),
        "w_gnn": flat(np.stack([blocks(g["L0_gnn_W_self"])[0, :, 0], blocks(g["L0_gnn_W_neigh"])[0, :, 0]], axis=1)),
        "w_mix": flat(blocks(np.concatenate([kqv(g["L0_mix_W_qkv"]), g["L0_mix_W_out"]]))),
        "w_sp": experts(e4(kqv(g[p + "sp_in_w"])), e4(g[p + "sp_out_w"])),
        "w_tp": experts(e4(np.concatenate([g[p + "tk_w"], g[p + "tq_w"], g[p + "tv_w"]], axis=1)), e4(g[p + "tp_w"])),
        "w_cr": flat(blocks(np.concatenate([kqv(g[p + "cross_in_w"]), g[p + "cross_out_w"]]))),
        "w_mlp": flat(np.concatenate([w1, w2], axis=1)),
        "vecs": np.ascontiguousarray(np.concatenate([columns(v) for v in (
            g["L0_gnn_b"], kqv_b(g["L0_mix_b_qkv"]), g["L0_mix_b_out"], g[p + "norm_s_w"], g[p + "norm_s_b"],
            g[p + "norm_t_w"], g[p + "norm_t_b"], kqv_b(g[p + "cross_in_b"]), g[p + "cross_out_b"],
            g[p + "norm_mlp_w"], g[p + "norm_mlp_b"], g[p + "mlp_b1"], g[p + "mlp_b2"], g[p + "router_b1"])], axis=1)),
        "v_sp": np.ascontiguousarray(np.concatenate([columns(kqv_b(g[p + "sp_in_b"])), columns(g[p + "sp_out_b"])], axis=2)),
        "v_tp": np.ascontiguousarray(np.concatenate([columns(g[p + n]) for n in ("tk_b", "tq_b", "tv_b", "tp_b")], axis=2)),
        "router_w1": np.ascontiguousarray(g[p + "router_w1"].T.reshape(FB, 128, 128).transpose(1, 0, 2)),
        "router_w2": np.ascontiguousarray(g[p + "router_w2"].T),
        "router_b2": np.ascontiguousarray(g[p + "router_b2"].reshape(1, -1)),
    }
    nc = bacc.Bacc("TRN2", target_bir_lowering=False, num_devices=1)
    aps = {n: nc.dram_tensor("in_" + n, a.shape, mybir.dt.from_np(a.dtype), kind="ExternalInput").ap()
           for n, a in arrays.items()}
    out = nc.dram_tensor("out", [NODES, D], F32, kind="ExternalOutput").ap()
    build(nc, aps, out)
    r = run_bass_kernel_spmd(nc, [{"in_" + n: a for n, a in arrays.items()}], core_ids=[0])
    return r.results[0]["out"]
```
